# Optimizing a Trainium2 kernel written in Bass

```python
import numpy as np
import jax
import jax.numpy as jnp

def _softmax(x, axis=-1):
    return jax.nn.softmax(x, axis=axis)

def _gelu(x):
    return jax.nn.gelu(x, approximate=True)

def _silu(x):
    return jax.nn.silu(x)

def _sigmoid(x):
    return jax.nn.sigmoid(x)

def _layernorm(x, axis=-1, eps=1e-05):
    m = jnp.mean(x, axis=axis, keepdims=True)
    v = jnp.var(x, axis=axis, keepdims=True)
    return (x - m) / jnp.sqrt(v + eps)

def _scatter_add(tgt, idx, src, axis=0):
    return tgt.at[idx].add(src)

def _segment_sum(src, seg, n):
    return jax.ops.segment_sum(src, seg, n)
kernel_name = 'mk_decoder_preln_d1_seqx_r4_a8357d'

def setup_inputs(seed: int=0):
    np.random.seed(seed)
    _w = jnp.asarray

    def _rec_inputs():
        import jax
        import jax.numpy as jnp
        _rk = jax.random.key(seed)
        x = 7.22e-05 + 1 * jax.random.normal(jax.random.fold_in(_rk, 1), (32, 100, 256), jnp.float32)
        _lenS = 100 - jax.random.randint(jax.random.fold_in(_rk, 7), (32,), 0, max(1, 100 // 4) + 1, jnp.int32)
        _lenS2 = 361 - jax.random.randint(jax.random.fold_in(_rk, 8), (32,), 0, max(1, 361 // 4) + 1, jnp.int32)
        _ctx_768P = jax.random.normal(jax.random.fold_in(_rk, 11), (32, 16, 192), jnp.float32)
        _ctx_768c = jax.random.dirichlet(jax.random.fold_in(_rk, 511), 0.3 * jnp.ones((16,), jnp.float32), (32, 361))
        _ctx_768t = jnp.einsum('bsk,bkd->bsd', _ctx_768c, _ctx_768P)
        _ctx_768t = _ctx_768t * jax.lax.rsqrt(jnp.mean(jnp.square(_ctx_768t)) + 1e-12) * 0.953939
        ctx_768 = -0.000191848 + 0.999787 * (_ctx_768t + 0.3 * jax.random.normal(jax.random.fold_in(_rk, 611), (32, 361, 192), jnp.float32))
        return (x, ctx_768)
    x, ctx_768 = _rec_inputs()

    def _L0_attn_setup():
        import jax, jax.numpy as jnp
        import numpy as np
        EPS = 1e-05
        key = jax.random.key(seed)
        ks = jax.random.split(key, 16)
        B, T, D = (8, 512, 256)
        Hh, KD, VD, LR, GLR = (4, 128, 256, 32, 64)
        s = 0.02
        w = lambda k, shape: jax.random.normal(k, shape, jnp.float32) * s
        return {'hidden_states': jax.random.normal(ks[0], (B, T, D), jnp.float32), 'mu_x': w(ks[1], (D,)), 'W_x1': w(ks[2], (5 * LR, D)), 'W_x2': w(ks[3], (D, 5 * LR)), 'x_bias': jnp.zeros((5, D), jnp.float32), 'W_r': w(ks[4], (KD, D)), 'W_k': w(ks[5], (KD, D)), 'W_v': w(ks[6], (VD, D)), 'W_g': w(ks[7], (VD, D)), 'A_w': w(ks[8], (GLR, D)), 'B_w': w(ks[9], (KD, GLR)), 'b_w': jnp.zeros((KD,), jnp.float32), 'bonus': w(ks[10], (Hh, KD // Hh)), 'gn_weight': jnp.ones((VD,), jnp.float32), 'gn_bias': jnp.zeros((VD,), jnp.float32), 'W_o': w(ks[11], (D, VD))}
    _L0_attn_all = _L0_attn_setup()
    _L0_attn_in = {k: v for k, v in _L0_attn_all.items() if k in ('mu_x', 'W_x1', 'W_x2', 'x_bias', 'W_r', 'W_k', 'W_v', 'W_g', 'A_w', 'B_w', 'b_w', 'bonus', 'gn_weight', 'gn_bias', 'W_o')}
    del _L0_attn_all

    def _L0_xattn_setup():
        import jax, jax.numpy as jnp
        import numpy as np
        NUM_HEADS = 16
        CLAMP = 10000.0
        key = jax.random.key(seed)
        ks = jax.random.split(key, 8)
        B, Nq, Nkv, Cq, Ckv = (4, 512, 512, 256, 192)
        s_q = 1.0 / np.sqrt(Cq)
        s_kv = 1.0 / np.sqrt(Ckv)
        return {'query': jax.random.normal(ks[0], (B, Nq, Cq), jnp.float32), 'key_value': jax.random.normal(ks[1], (B, Nkv, Ckv), jnp.float32), 'Wq': jax.random.normal(ks[2], (Cq, Cq), jnp.float32) * s_q, 'bq': jnp.zeros((Cq,), jnp.float32), 'Wk': jax.random.normal(ks[3], (Ckv, Cq), jnp.float32) * s_kv, 'bk': jnp.zeros((Cq,), jnp.float32), 'Wv': jax.random.normal(ks[4], (Ckv, Cq), jnp.float32) * s_kv, 'bv': jnp.zeros((Cq,), jnp.float32), 'Wo': jax.random.normal(ks[5], (Cq, Cq), jnp.float32) * s_q, 'bo': jnp.zeros((Cq,), jnp.float32)}
    _L0_xattn_all = _L0_xattn_setup()
    _L0_xattn_in = {k: v for k, v in _L0_xattn_all.items() if k in ('Wq', 'bq', 'Wk', 'bk', 'Wv', 'bv', 'Wo', 'bo')}
    del _L0_xattn_all

    def _L0_ffn_setup():
        import jax, jax.numpy as jnp
        import numpy as np
        B, T, C = (4, 512, 256)
        E, F, K = (8, 512, 2)
        key = jax.random.key(seed)
        k0, k1, k2, k3 = jax.random.split(key, 4)
        s = lambda d: 1.0 / np.sqrt(d)
        x = jax.random.normal(k0, (B, T, C), dtype=jnp.float32)
        Wr = jax.random.normal(k1, (E, C), dtype=jnp.float32) * s(C)
        W1 = jax.random.normal(k2, (E, 2 * F, C), dtype=jnp.float32) * s(C)
        W2 = jax.random.normal(k3, (E, C, F), dtype=jnp.float32) * s(F)
        return {'x': x, 'Wr': Wr, 'W1': W1, 'W2': W2}
    _L0_ffn_all = _L0_ffn_setup()
    _L0_ffn_in = {k: v for k, v in _L0_ffn_all.items() if k in ('Wr', 'W1', 'W2')}
    del _L0_ffn_all
    return {'x': x, 'ctx_768': ctx_768, 'L0_attn_mu_x': _L0_attn_in['mu_x'], 'L0_attn_W_x1': _L0_attn_in['W_x1'], 'L0_attn_W_x2': _L0_attn_in['W_x2'], 'L0_attn_x_bias': _L0_attn_in['x_bias'], 'L0_attn_W_r': _L0_attn_in['W_r'], 'L0_attn_W_k': _L0_attn_in['W_k'], 'L0_attn_W_v': _L0_attn_in['W_v'], 'L0_attn_W_g': _L0_attn_in['W_g'], 'L0_attn_A_w': _L0_attn_in['A_w'], 'L0_attn_B_w': _L0_attn_in['B_w'], 'L0_attn_b_w': _L0_attn_in['b_w'], 'L0_attn_bonus': _L0_attn_in['bonus'], 'L0_attn_gn_weight': _L0_attn_in['gn_weight'], 'L0_attn_gn_bias': _L0_attn_in['gn_bias'], 'L0_attn_W_o': _L0_attn_in['W_o'], 'L0_xattn_Wq': _L0_xattn_in['Wq'], 'L0_xattn_bq': _L0_xattn_in['bq'], 'L0_xattn_Wk': _L0_xattn_in['Wk'], 'L0_xattn_bk': _L0_xattn_in['bk'], 'L0_xattn_Wv': _L0_xattn_in['Wv'], 'L0_xattn_bv': _L0_xattn_in['bv'], 'L0_xattn_Wo': _L0_xattn_in['Wo'], 'L0_xattn_bo': _L0_xattn_in['bo'], 'L0_ffn_Wr': _L0_ffn_in['Wr'], 'L0_ffn_W1': _L0_ffn_in['W1'], 'L0_ffn_W2': _L0_ffn_in['W2']}

def reference(x, ctx_768, L0_attn_mu_x, L0_attn_W_x1, L0_attn_W_x2, L0_attn_x_bias, L0_attn_W_r, L0_attn_W_k, L0_attn_W_v, L0_attn_W_g, L0_attn_A_w, L0_attn_B_w, L0_attn_b_w, L0_attn_bonus, L0_attn_gn_weight, L0_attn_gn_bias, L0_attn_W_o, L0_xattn_Wq, L0_xattn_bq, L0_xattn_Wk, L0_xattn_bk, L0_xattn_Wv, L0_xattn_bv, L0_xattn_Wo, L0_xattn_bo, L0_ffn_Wr, L0_ffn_W1, L0_ffn_W2):
    import jax
    import jax.numpy as jnp

    def _L0_attn_ref(hidden_states, mu_x, W_x1, W_x2, x_bias, W_r, W_k, W_v, W_g, A_w, B_w, b_w, bonus, gn_weight, gn_bias, W_o):
        import jax, jax.numpy as jnp
        import numpy as np
        EPS = 1e-05
        B, T, D = hidden_states.shape
        Hh = bonus.shape[0]
        x = hidden_states
        shifted = jnp.pad(x, ((0, 0), (1, 0), (0, 0)))[:, :T]
        delta = shifted - x
        lr = W_x1.shape[0] // 5
        z = jnp.tanh((x + delta * mu_x) @ W_x1.T).reshape(B, T, 5, lr)
        mus = jnp.einsum('blnr,dnr->blnd', z, W_x2.reshape(D, 5, lr)) + x_bias
        r_mu, w_mu, k_mu, v_mu, g_mu = (mus[:, :, i] for i in range(5))
        r = (x + delta * r_mu) @ W_r.T
        w = jnp.tanh((x + delta * w_mu) @ A_w.T) @ B_w.T + b_w
        k = (x + delta * k_mu) @ W_k.T
        v = (x + delta * v_mu) @ W_v.T
        g = (x + delta * g_mu) @ W_g.T
        K = W_r.shape[0] // Hh
        V = W_v.shape[0] // Hh
        r = r.reshape(B, T, Hh, K)
        k = k.reshape(B, T, Hh, K)
        w = -jnp.exp(w.reshape(B, T, Hh, K))
        v = v.reshape(B, T, Hh, V)
        u = bonus

        def step(S, inp):
            q_t, k_t, v_t, w_t = inp
            kv = k_t[..., :, None] * v_t[..., None, :]
            o_t = jnp.einsum('bhk,bhkv->bhv', q_t, S + u[None, :, :, None] * kv)
            S = jnp.exp(w_t)[..., None] * S + kv
            return (S, o_t)
        S0 = jnp.zeros((B, Hh, K, V), dtype=x.dtype)
        xs = (jnp.swapaxes(r, 0, 1), jnp.swapaxes(k, 0, 1), jnp.swapaxes(v, 0, 1), jnp.swapaxes(w, 0, 1))
        _, o = jax.lax.scan(step, S0, xs)
        o = jnp.swapaxes(o, 0, 1)
        mean = o.mean(-1, keepdims=True)
        var = o.var(-1, keepdims=True)
        o = (o - mean) / jnp.sqrt(var + EPS)
        o = o.reshape(B, T, Hh * V) * gn_weight + gn_bias
        o = o * jax.nn.silu(g)
        return o @ W_o.T

    def _L0_xattn_ref(query, key_value, Wq, bq, Wk, bk, Wv, bv, Wo, bo):
        import jax, jax.numpy as jnp
        import numpy as np
        NUM_HEADS = 16
        CLAMP = 10000.0
        B, Nq, Cq = query.shape
        Nkv = key_value.shape[1]
        H = NUM_HEADS
        D = Cq // H
        scale = D ** (-0.5)
        q = (query @ Wq + bq).reshape(B, Nq, H, D).transpose(0, 2, 1, 3)
        k = (key_value @ Wk + bk).reshape(B, Nkv, H, D).transpose(0, 2, 1, 3)
        v = (key_value @ Wv + bv).reshape(B, Nkv, H, D).transpose(0, 2, 1, 3)
        attn = jnp.einsum('bhqd,bhkd->bhqk', q, k) * scale
        attn = jnp.clip(attn, -CLAMP, CLAMP)
        attn = jax.nn.softmax(attn, axis=-1)
        attn = jnp.where(jnp.any(jnp.isnan(attn)), jnp.asarray(1.0 / Nkv, attn.dtype), attn)
        x = jnp.einsum('bhqk,bhkd->bqhd', attn, v).reshape(B, Nq, Cq)
        return x @ Wo + bo

    def _L0_ffn_ref(x, Wr, W1, W2):
        import jax, jax.numpy as jnp
        import numpy as np
        B, T, C = (4, 512, 256)
        E, F, K = (8, 512, 2)
        Bb, Tt, Cc = x.shape
        flat = x.reshape(-1, Cc)
        N = flat.shape[0]
        logits = flat @ Wr.T
        weights, ids = jax.lax.top_k(logits, K)
        weights = jax.nn.softmax(weights, axis=-1)
        rows = jnp.arange(N)[:, None]
        router_weights = jnp.zeros((N, E), dtype=flat.dtype).at[rows, ids].add(weights)
        h = jnp.einsum('nc,efc->nef', flat, W1)
        val, gate = (h[..., :F], h[..., F:])
        act = val * jax.nn.silu(gate)
        expert_outputs = jnp.einsum('nef,ecf->nec', act, W2)
        out = jnp.einsum('nec,ne->nc', expert_outputs, router_weights)
        return out.reshape(Bb, Tt, Cc)
    x = x + _L0_attn_ref(_layernorm(x, axis=-1), L0_attn_mu_x, L0_attn_W_x1, L0_attn_W_x2, L0_attn_x_bias, L0_attn_W_r, L0_attn_W_k, L0_attn_W_v, L0_attn_W_g, L0_attn_A_w, L0_attn_B_w, L0_attn_b_w, L0_attn_bonus, L0_attn_gn_weight, L0_attn_gn_bias, L0_attn_W_o)
    x = x + _L0_xattn_ref(_layernorm(x, axis=-1), ctx_768, L0_xattn_Wq, L0_xattn_bq, L0_xattn_Wk, L0_xattn_bk, L0_xattn_Wv, L0_xattn_bv, L0_xattn_Wo, L0_xattn_bo)
    x = x + _L0_ffn_ref(_layernorm(x, axis=-1), L0_ffn_Wr, L0_ffn_W1, L0_ffn_W2)
    return x

_drawn_inputs = setup_inputs


def setup_inputs(seed=0):
    import zlib

    import numpy as np

    out = dict(_drawn_inputs(seed))
    spreads = {'L0_attn_x_bias': (0.0, 0.1),
     'L0_attn_b_w': (0.0, 0.518),
     'L0_attn_gn_weight': (1.0, 0.536),
     'L0_attn_gn_bias': (0.0, 0.361),
     'L0_xattn_bq': (0.0, 0.1),
     'L0_xattn_bk': (0.0, 0.8),
     'L0_xattn_bv': (0.0, 0.1),
     'L0_xattn_bo': (0.0, 0.1)}
    factors = {'L0_attn_mu_x': 8.0,
     'L0_attn_W_x1': 2.728,
     'L0_attn_W_x2': 3.111,
     'L0_attn_A_w': 6.594,
     'L0_attn_B_w': 6.872,
     'L0_attn_bonus': 5.673}
    for name, (base, spread) in spreads.items():
        noise = np.random.default_rng([zlib.crc32(name.encode()), seed]).standard_normal(out[name].shape)
        drawn = base * np.exp(spread * noise) if base else spread * noise
        out[name] = jnp.asarray(drawn.astype(out[name].dtype))
    for name, factor in factors.items():
        out[name] = (out[name] * factor).astype(out[name].dtype)
    return out
```

```python
from contextlib import ExitStack

import concourse.bass as bass
from concourse import mybir

ALU = mybir.AluOpType
ACT = mybir.ActivationFunctionType
AX = mybir.AxisListType
F32 = mybir.dt.float32
BF16 = mybir.dt.bfloat16
U8 = mybir.dt.uint8
U32 = mybir.dt.uint32
I32 = mybir.dt.int32

BATCH, T, D = 32, 100, 256
EPS = 1e-5
G = 4
GROUPS = BATCH // G
GT = G * T
CC = D // 128
RH, RK, RV = 4, 32, 64
TP = 128
BRANCHES = 5
LEVELS = 8
S = 361
KC = 96
NH = 16
KEYS = (121, 120, 120)
KEY0 = (0, 121, 241)
CLAMP = 10000.0
E = 8
F = 512
FC = F // 128
EXPERT_TILES = BATCH * T // 128
TILES = (2 * BATCH * T + E * 127) // 128


def stage_mixer(nc, w, x, x1):
    with ExitStack() as ctx:
        def sb(name, shape, dt=F32):
            return ctx.enter_context(nc.sbuf_tensor(name, shape, dt))

        def sem(name):
            return ctx.enter_context(nc.semaphore(name))

        w_x1 = sb("w_x1", [128, CC, 256])
        w_x2 = sb("w_x2", [128, BRANCHES, 256])
        w_r = sb("w_r", [128, CC, 128])
        w_k = sb("w_k", [128, CC, 128])
        w_a = sb("w_a", [128, CC, 128])
        w_b = sb("w_b", [128, 128])
        w_v = sb("w_v", [128, CC, 256])
        w_g = sb("w_g", [128, CC, 256])
        w_o = sb("w_o", [128, CC, 256])
        mu_x = sb("mu_x", [128, CC])
        mix_bias = sb("mix_bias", [128, BRANCHES, CC])
        b_w = sb("b_w", [128, 1])
        bonus = sb("bonus", [128, 1])
        gn_w = sb("gn_w", [T, 256])
        gn_b = sb("gn_b", [T, 256])
        masks = sb("masks", [T, LEVELS - 1, T], I32)
        ident = sb("ident", [T, T])
        power = sb("power", [T, 16])
        eps = sb("eps", [T, 16])

        stats = sb("stats", [T, G, 6])
        mean_var = sb("mean_var", [T, G, 2])
        rstd = sb("rstd", [T, G])
        xn = sb("xn", [T, G, D])
        xn_t = sb("xn_t", [128, CC, G, T + 1])
        delta = sb("delta", [128, CC, G, T])
        xz = sb("xz", [128, CC, G, T])
        z = sb("z", [128, 2, GT])
        part = sb("part", [128, 2, CC, GT])
        mixed = sb("mixed", [128, 2, CC, GT])
        wa = sb("wa", [128, GT])
        rate = sb("rate", [128, GT])
        q = sb("q", [128, G, TP])
        k = sb("k", [128, G, TP])
        decay = sb("decay", [128, G, TP])
        total = sb("total", [128, 2, G * TP // 2])
        q_heads = sb("q_heads", [128, 2, RH, GT])
        attn = sb("attn", [T, G, RH, T])
        val = sb("val", [T, G, D])
        tanh_g = sb("tanh_g", [T, G, D])
        half_g = sb("half_g", [T, G, D])
        gate = sb("gate", [T, G, D])
        gn_stats = sb("gn_stats", [T, G * RH, 6])
        gn_mv = sb("gn_mv", [T, G * RH, 2])
        gn_rstd = sb("gn_rstd", [T, G * RH])
        normed = sb("normed", [T, G, D])
        normed_t = sb("normed_t", [128, CC, GT])

        bank_a = [ctx.enter_context(nc.psum_tensor(f"bank_a{i}", [128, 512], F32)) for i in range(4)]
        bank_t = [ctx.enter_context(nc.psum_tensor(f"bank_t{i}", [128, 512], F32)) for i in range(4)]

        x_loaded = sem("x_loaded")
        w_loaded = sem("w_loaded")
        consts = sem("consts")
        waited = sem("waited")
        stats_done = sem("stats_done")
        mv_done = sem("mv_done")
        eps_added = sem("eps_added")
        rstd_done = sem("rstd_done")
        xn_done = sem("xn_done")
        xn_turned = sem("xn_turned")
        xn_t_done = sem("xn_t_done")
        delta_done = sem("delta_done")
        xz_done = sem("xz_done")
        z_summed = sem("z_summed")
        z_done = sem("z_done")
        lora_summed = sem("lora_summed")
        part_done = sem("part_done")
        mixed_done = sem("mixed_done")
        r_summed = sem("r_summed")
        a_summed = sem("a_summed")
        k_summed = sem("k_summed")
        w_summed = sem("w_summed")
        v_summed = sem("v_summed")
        g_summed = sem("g_summed")
        q_done = sem("q_done")
        wa_done = sem("wa_done")
        k_done = sem("k_done")
        rate_done = sem("rate_done")
        decay_done = sem("decay_done")
        val_done = sem("val_done")
        gate_in = sem("gate_in")
        gate_done = sem("gate_done")
        q_decayed = sem("q_decayed")
        total_done = sem("total_done")
        k_decayed = sem("k_decayed")
        heads_act = sem("heads_act")
        heads_dve = sem("heads_dve")
        level_summed = sem("level_summed")
        attn_done = sem("attn_done")
        o_summed = sem("o_summed")
        gn_stats_done = sem("gn_stats_done")
        gn_mv_done = sem("gn_mv_done")
        gn_eps = sem("gn_eps")
        gn_rstd_done = sem("gn_rstd_done")
        centred = sem("centred")
        scaled = sem("scaled")
        weighted = sem("weighted")
        shifted = sem("shifted")
        gated = sem("gated")
        o_turned = sem("o_turned")
        normed_t_done = sem("normed_t_done")
        out_summed = sem("out_summed")
        x1_done = sem("x1_done")

        WEIGHTS = [(w_x1, w["x1"]), (w_x2, w["x2"]), (w_r, w["r"]), (w_k, w["k"]), (w_a, w["a"]),
                   (w_b, w["b"]), (w_v, w["v"]), (w_g, w["g"]), (w_o, w["o"]), (mu_x, w["mu_x"]),
                   (mix_bias, w["x_bias"]), (b_w, w["b_w"]), (bonus, w["bonus"]), (gn_w, w["gn_w"]),
                   (gn_b, w["gn_b"]), (masks, w["masks"]), (ident, w["ident"])]
        CONSTS = 10
        block = ctx.enter_context(nc.Block())

        @block.sync
        def _(sp):
            for g in range(GROUPS):
                if g:
                    sp.wait_ge(x_loaded, 16 * g)
                sp.dma_start(x1[:, g * G:(g + 1) * G, :],
                             x[g * G:(g + 1) * G].rearrange("b t d -> t b d")).then_inc(x_loaded, 16)
                if g == 0:
                    for tile, src in WEIGHTS:
                        sp.dma_start(tile[:], src).then_inc(w_loaded, 16)

        @block.gpsimd
        def _(pool):
            pool.memset(power[:], -0.5).then_inc(consts, 1)
            pool.memset(eps[:], EPS).then_inc(consts, 1)
            pool.memset(xn_t[:, :, :, 0:1], 0.0).then_inc(consts, 1)
            pool.memset(q[:], 0.0).then_inc(consts, 1)
            pool.memset(k[:], 0.0).then_inc(consts, 1)
            pool.memset(decay[:], 1.0).then_inc(consts, 1)
            pool.memset(q_heads[:, 0], 0.0).then_inc(consts, 1)
            pool.memset(q_heads[:, 1], 0.0).then_inc(consts, 1)
            pool.memset(attn[:], 0.0).then_inc(consts, 1)
            pool.memset(total[:], 1.0).then_inc(consts, 1)
            pool.wait_ge(consts, CONSTS)
            with pool.Fori(0, GROUPS) as g:
                pool.wait_ge(mv_done, (g + 1) * G)
                pool.tensor_tensor(rstd[:], mean_var[:, :, 1], eps[:, 0:G], ALU.add).then_inc(eps_added, 1)
                pool.wait_ge(eps_added, g + 1)
                pool.tensor_tensor(rstd[:], rstd[:], power[:, 0:G], ALU.pow).then_inc(rstd_done, 1)
                for n in range(BRANCHES * CC):
                    i, c = n // CC, n % CC
                    pool.wait_ge(part_done, g * BRANCHES * CC + n + 1)
                    if n == 2 * CC:
                        pool.wait_ge(r_summed, g + 1)
                    if n == 3 * CC:
                        pool.wait_ge(a_summed, g + 1)
                    if n == 4 * CC:
                        pool.wait_ge(k_summed, g + 1)
                    pool.tensor_tensor(mixed[:, i % 2, c].rearrange("p (b t) -> p b t", b=G),
                                       part[:, i % 2, c].rearrange("p (b t) -> p b t", b=G),
                                       xn_t[:, c, :, 1:T + 1], ALU.add).then_inc(mixed_done, 1)
                pool.wait_ge(gn_mv_done, (g + 1) * G * RH)
                pool.tensor_tensor(gn_rstd[:], gn_mv[:, :, 1], eps[:], ALU.add).then_inc(gn_eps, 1)
                pool.wait_ge(gn_eps, g + 1)
                pool.tensor_tensor(gn_rstd[:], gn_rstd[:], power[:], ALU.pow).then_inc(gn_rstd_done, 1)
                pool.wait_ge(gate_done, (g + 1) * 2)
                for j in range(G):
                    pool.wait_ge(scaled, g * 2 + j // 2 + 1)
                    pool.tensor_tensor(normed[:, j], normed[:, j], gn_w[:], ALU.mult).then_inc(weighted, 1)
                    pool.wait_ge(weighted, g * G + j + 1)
                    pool.tensor_tensor(normed[:, j], normed[:, j], gn_b[:], ALU.add).then_inc(shifted, 1)
                    pool.wait_ge(shifted, g * G + j + 1)
                    pool.tensor_tensor(normed[:, j], normed[:, j], gate[:, j], ALU.mult).then_inc(gated, 1)

        @block.scalar
        def _(act):
            act.wait_ge(consts, CONSTS)
            act.wait_ge(w_loaded, 16 * len(WEIGHTS))
            with act.Fori(0, GROUPS) as g:
                for c in range(CC):
                    act.wait_ge(xn_turned, g * CC + c + 1)
                    act.activation(xn_t[:, c, :, 1:T + 1],
                                   bank_t[c][:, 0:GT].rearrange("p (b t) -> p b t", b=G),
                                   ACT.Copy).then_inc(xn_t_done, 1)
                for m in range(2):
                    act.wait_ge(z_summed, g * 2 + m + 1)
                    act.activation(z[:, m], bank_t[2 + m][:, 0:GT], ACT.Tanh).then_inc(z_done, 1)
                act.wait_ge(r_summed, g + 1)
                act.activation(q[:, :, 0:T], bank_a[0][:, 0:GT].rearrange("p (b t) -> p b t", b=G),
                               ACT.Copy).then_inc(q_done, 1)
                act.wait_ge(a_summed, g + 1)
                act.activation(wa[:], bank_a[1][:, 0:GT], ACT.Tanh).then_inc(wa_done, 1)
                act.wait_ge(k_summed, g + 1)
                act.activation(k[:, :, 0:T], bank_a[2][:, 0:GT].rearrange("p (b t) -> p b t", b=G),
                               ACT.Copy).then_inc(k_done, 1)
                act.wait_ge(w_summed, g + 1)
                act.activation(rate[:], bank_a[3][:, 0:GT], ACT.Exp, bias=b_w[:, 0:1]).then_inc(rate_done, 1)
                act.wait_ge(rate_done, g + 1)
                act.activation(decay[:, :, 0:T], rate[:].rearrange("p (b t) -> p b t", b=G), ACT.Exp,
                               scale=-1.0).then_inc(decay_done, 1)
                for p in range(2):
                    act.wait_ge(v_summed, g * 2 + p + 1)
                    act.activation(val[:, 2 * p:2 * p + 2], bank_a[p][0:T].rearrange("p (b d) -> p b d", b=2),
                                   ACT.Copy).then_inc(val_done, 1)
                for p in range(2):
                    act.wait_ge(g_summed, g * 2 + p + 1)
                    src = bank_a[2 + p][0:T].rearrange("p (b d) -> p b d", b=2)
                    act.activation(tanh_g[:, 2 * p:2 * p + 2], src, ACT.Tanh, scale=0.5)
                    act.activation(half_g[:, 2 * p:2 * p + 2], src, ACT.Copy, scale=0.5).then_inc(gate_in, 1)
                for lv in range(LEVELS):
                    if lv >= 2:
                        act.wait_ge(q_decayed, g * (LEVELS - 2) + lv - 1)
                        act.wait_ge(level_summed, g * LEVELS * G + (lv - 1) * G)
                    for h in range(2):
                        rows = slice(RK * h, RK * h + RK)
                        act.activation(q_heads[rows, lv % 2, h].rearrange("p (b t) -> p b t", b=G),
                                       q[rows, :, 0:T], ACT.Copy,
                                       scale=bonus[rows, 0:1] if lv == 0 else 1.0).then_inc(heads_act, 1)
                for c in range(CC):
                    act.wait_ge(o_turned, g * CC + c + 1)
                    act.activation(normed_t[:, c], bank_t[2 + c][:, 0:GT], ACT.Copy).then_inc(normed_t_done, 1)

        @block.vector
        def _(dve):
            dve.wait_ge(consts, CONSTS)
            dve.wait_ge(w_loaded, 16 * len(WEIGHTS))
            with dve.Fori(0, GROUPS) as g:
                dve.wait_ge(x_loaded, (g + 1) * 16)
                for j in range(G):
                    dve.bn_stats(stats[:, j], x1[:, g * G + j, :]).then_inc(stats_done, 1)
                for j in range(G):
                    dve.wait_ge(stats_done, g * G + j + 1)
                    dve.sem_inc(waited, 1)
                    dve.bn_aggr(mean_var[:, j], stats[:, j]).then_inc(mv_done, 1)
                dve.wait_ge(rstd_done, g + 1)
                for j in range(G):
                    dve.tensor_scalar(xn[:, j], x1[:, g * G + j, :], mean_var[:, j, 0:1], rstd[:, j:j + 1],
                                      ALU.subtract, ALU.mult).then_inc(xn_done, 1)
                dve.wait_ge(xn_t_done, (g + 1) * CC)
                dve.tensor_tensor(delta[:].rearrange("p c b t -> p (c b) t"),
                                  xn_t[:, :, :, 0:T].rearrange("p c b t -> p (c b) t"),
                                  xn_t[:, :, :, 1:T + 1].rearrange("p c b t -> p (c b) t"),
                                  ALU.subtract).then_inc(delta_done, 1)
                dve.wait_ge(delta_done, g + 1)
                for c in range(CC):
                    dve.scalar_tensor_tensor(xz[:, c], delta[:, c], mu_x[:, c:c + 1], xn_t[:, c, :, 1:T + 1],
                                             ALU.mult, ALU.add).then_inc(xz_done, 1)
                for n in range(BRANCHES * CC):
                    i, c = n // CC, n % CC
                    dve.wait_ge(lora_summed, g * BRANCHES * CC + n + 1)
                    if n >= 2 * CC:
                        dve.wait_ge(mixed_done, g * BRANCHES * CC + n - 2 * CC + 1)
                    dve.scalar_tensor_tensor(part[:, i % 2, c], bank_t[n % 4][:, 0:GT],
                                             mix_bias[:, i, c:c + 1],
                                             delta[:, c].rearrange("p b t -> p (b t)"),
                                             ALU.add, ALU.mult).then_inc(part_done, 1)
                for lv in range(LEVELS + 1):
                    if lv == 0:
                        dve.wait_ge(q_done, g + 1)
                    if 2 <= lv < LEVELS:
                        half = 1 << (lv - 2)
                        nseg = G * TP // (2 * half)
                        seg = "p (s two h) -> p s two h"
                        qv = q[:].rearrange("p b t -> p (b t)").rearrange(seg, two=2, h=half)
                        kv = k[:].rearrange("p b t -> p (b t)").rearrange(seg, two=2, h=half)
                        if half == 1:
                            dve.wait_ge(decay_done, g + 1)
                            dve.wait_ge(k_done, g + 1)
                            tot = decay[:].rearrange("p b t -> p (b t)")
                        else:
                            dve.wait_ge(total_done, g * (LEVELS - 2) + lv - 2)
                            tot = total[:, lv % 2, 0:2 * nseg]
                        tv = tot.rearrange("p (s two) -> p s two", two=2)
                        dve.wait_ge(heads_act, g * LEVELS * 2 + lv * 2)
                        dve.wait_ge(heads_dve, g * LEVELS * 2 + lv * 2)
                        dve.tensor_tensor(qv[:, :, 1], qv[:, :, 1], tv[:, :, 0:1].to_broadcast([128, nseg, half]),
                                          ALU.mult).then_inc(q_decayed, 1)
                        if lv > 2:
                            dve.wait_ge(k_decayed, g * (LEVELS - 2) + lv - 2)
                        dve.tensor_tensor(total[:, (lv + 1) % 2, 0:nseg], tv[:, :, 0], tv[:, :, 1],
                                          ALU.mult).then_inc(total_done, 1)
                        dve.wait_ge(q_decayed, g * (LEVELS - 2) + lv - 1)
                        dve.wait_ge(level_summed, g * LEVELS * G + (lv - 1) * G)
                    if lv < LEVELS:
                        for h in range(2, RH):
                            rows = slice(RK * h, RK * h + RK)
                            dst = q_heads[rows, lv % 2, h].rearrange("p (b t) -> p b t", b=G)
                            if lv == 0:
                                dve.tensor_scalar(dst, q[rows, :, 0:T], bonus[rows, 0:1], None,
                                                  ALU.mult).then_inc(heads_dve, 1)
                            else:
                                dve.tensor_copy(dst, q[rows, :, 0:T]).then_inc(heads_dve, 1)
                    if 2 <= lv < LEVELS:
                        dve.wait_ge(level_summed, (g * LEVELS + lv) * G)
                        dve.tensor_tensor(kv[:, :, 0], kv[:, :, 0], tv[:, :, 1:2].to_broadcast([128, nseg, half]),
                                          ALU.mult).then_inc(k_decayed, 1)
                    if lv == 1:
                        for p in range(2):
                            dve.wait_ge(gate_in, g * 2 + p + 1)
                            dve.scalar_tensor_tensor(gate[:, 2 * p:2 * p + 2], tanh_g[:, 2 * p:2 * p + 2], 1.0,
                                                     half_g[:, 2 * p:2 * p + 2], ALU.add,
                                                     ALU.mult).then_inc(gate_done, 1)
                    if lv >= 1:
                        for j in range(G):
                            dve.wait_ge(level_summed, g * LEVELS * G + (lv - 1) * G + j + 1)
                            if lv == LEVELS:
                                dve.tensor_copy(attn[0:64, j, :, 64:T],
                                                bank_a[j][0:64, 0:GT].rearrange("p (h t) -> p h t", h=RH)[:, :, 64:T]
                                                ).then_inc(attn_done, 1)
                            else:
                                dve.sem_inc(waited, 1)
                                dve.copy_predicated(attn[:, j],
                                                    masks[:, lv - 1:lv, :].to_broadcast([T, RH, T]),
                                                    bank_a[j][0:T, 0:GT].rearrange("p (h t) -> p h t", h=RH)
                                                    ).then_inc(attn_done, 1)
                for n in range(G * RH):
                    dve.wait_ge(o_summed, g * 2 + n // 8 + 1)
                    dve.bn_stats(gn_stats[:, n], bank_t[n // 8][0:T, (n % 8) * RV:(n % 8 + 1) * RV]
                                 ).then_inc(gn_stats_done, 1)
                for n in range(G * RH):
                    dve.wait_ge(gn_stats_done, g * G * RH + n + 1)
                    dve.sem_inc(waited, 1)
                    dve.bn_aggr(gn_mv[:, n], gn_stats[:, n]).then_inc(gn_mv_done, 1)
                dve.wait_ge(gn_mv_done, (g + 1) * G * RH)
                for p in range(2):
                    out = normed[:, 2 * p:2 * p + 2].rearrange("p b (h v) -> p (b h) v", h=RH)
                    dve.tensor_tensor(out, bank_t[p][0:T].rearrange("p (n v) -> p n v", v=RV),
                                      gn_mv[:, 8 * p:8 * p + 8, 0:1].to_broadcast([T, 8, RV]),
                                      ALU.subtract).then_inc(centred, 1)
                dve.wait_ge(gn_rstd_done, g + 1)
                for p in range(2):
                    out = normed[:, 2 * p:2 * p + 2].rearrange("p b (h v) -> p (b h) v", h=RH)
                    dve.wait_ge(centred, g * 2 + p + 1)
                    dve.tensor_tensor(out, out, gn_rstd[:, 8 * p:8 * p + 8].unsqueeze(2).to_broadcast([T, 8, RV]),
                                      ALU.mult).then_inc(scaled, 1)
                for p in range(2):
                    dve.wait_ge(out_summed, g * 2 + p + 1)
                    res = x1[:, bass.ds(g * G + 2 * p, 2), :].rearrange("p b d -> p (b d)")
                    dve.tensor_tensor(res, res, bank_t[p][0:T], ALU.add).then_inc(x1_done, 1)
                dve.wait_ge(x1_done, (g + 1) * 2)

        @block.tensor
        def _(pe):
            pe.wait_ge(w_loaded, 16 * len(WEIGHTS))
            pe.wait_ge(consts, CONSTS)

            def project(g, dst, weight, slot, done):
                for c in range(CC):
                    mm = pe.matmul(dst[:, 0:GT], weight[:, c], mixed[:, slot, c], start=(c == 0), stop=(c == CC - 1))
                mm.then_inc(done, 1)

            def project_rows(g, banks, weight, slot, done):
                for p in range(2):
                    for j in (2 * p, 2 * p + 1):
                        for c in range(CC):
                            mm = pe.matmul(banks[p][0:T, (j % 2) * D:(j % 2 + 1) * D],
                                           mixed[:, slot, c, j * T:(j + 1) * T], weight[:, c],
                                           start=(c == 0), stop=(c == CC - 1))
                    mm.then_inc(done, 1)

            with pe.Fori(0, GROUPS) as g:
                def lora(i):
                    for c in range(CC):
                        n = i * CC + c
                        if n >= 4:
                            pe.wait_ge(part_done, g * BRANCHES * CC + n - 3)
                        mm = pe.matmul(bank_t[n % 4][:, 0:GT], w_x2[:, i, c * 128:(c + 1) * 128], z[:, i // 4],
                                       start=True, stop=True)
                        mm.then_inc(lora_summed, 1)

                def mixed_ready(i):
                    pe.wait_ge(mixed_done, g * BRANCHES * CC + (i + 1) * CC)

                pe.wait_ge(xn_done, (g + 1) * G)
                for c in range(CC):
                    for j in range(G):
                        mm = pe.transpose(bank_t[c][:, j * T:(j + 1) * T], xn[:, j, c * 128:(c + 1) * 128], ident[:])
                    mm.then_inc(xn_turned, 1)
                pe.wait_ge(xz_done, (g + 1) * CC)
                for m in range(2):
                    for c in range(CC):
                        mm = pe.matmul(bank_t[2 + m][:, 0:GT], w_x1[:, c, m * 128:(m + 1) * 128],
                                       xz[:, c].rearrange("p b t -> p (b t)"), start=(c == 0), stop=(c == CC - 1))
                    mm.then_inc(z_summed, 1)
                pe.wait_ge(z_done, (g + 1) * 2)
                lora(0)
                lora(1)
                mixed_ready(0)
                project(g, bank_a[0], w_r, 0, r_summed)
                lora(2)
                mixed_ready(1)
                project(g, bank_a[1], w_a, 1, a_summed)
                lora(3)
                mixed_ready(2)
                project(g, bank_a[2], w_k, 0, k_summed)
                lora(4)
                pe.wait_ge(wa_done, g + 1)
                pe.matmul(bank_a[3][:, 0:GT], w_b[:], wa[:], start=True, stop=True).then_inc(w_summed, 1)
                mixed_ready(3)
                pe.wait_ge(q_done, g + 1)
                project_rows(g, bank_a[0:2], w_v, 1, v_summed)
                mixed_ready(4)
                pe.wait_ge(k_done, g + 1)
                pe.wait_ge(rate_done, g + 1)
                project_rows(g, bank_a[2:4], w_g, 0, g_summed)
                for lv in range(LEVELS):
                    pe.wait_ge(heads_act, g * LEVELS * 2 + (lv + 1) * 2)
                    pe.wait_ge(heads_dve, g * LEVELS * 2 + (lv + 1) * 2)
                    if lv == 0:
                        pe.wait_ge(val_done, (g + 1) * 2)
                        pe.wait_ge(gate_in, (g + 1) * 2)
                    if lv >= 2:
                        pe.wait_ge(k_decayed, g * (LEVELS - 2) + lv - 1)
                    for j in range(G):
                        if lv >= 1:
                            pe.wait_ge(attn_done, g * LEVELS * G + (lv - 1) * G + j + 1)
                        pe.matmul(bank_a[j][0:T, 0:GT], k[:, j, 0:T], q_heads[:, lv % 2, :, j * T:(j + 1) * T],
                                  start=True, stop=True).then_inc(level_summed, 1)
                pe.wait_ge(attn_done, (g + 1) * LEVELS * G)
                pe.wait_ge(part_done, (g + 1) * BRANCHES * CC)
                for p in range(2):
                    for j in (2 * p, 2 * p + 1):
                        for h in range(RH):
                            mm = pe.matmul(bank_t[p][0:T, (j % 2) * D + h * RV:(j % 2) * D + (h + 1) * RV],
                                           attn[:, j, h, :], val[:, j, h * RV:(h + 1) * RV], start=True, stop=True)
                    mm.then_inc(o_summed, 1)
                for c in range(CC):
                    for j in range(G):
                        if c == 0:
                            pe.wait_ge(gated, g * G + j + 1)
                        mm = pe.transpose(bank_t[2 + c][:, j * T:(j + 1) * T], normed[:, j, c * 128:(c + 1) * 128],
                                          ident[:])
                    mm.then_inc(o_turned, 1)
                pe.wait_ge(normed_t_done, (g + 1) * CC)
                for p in range(2):
                    for j in (2 * p, 2 * p + 1):
                        for c in range(CC):
                            mm = pe.matmul(bank_t[p][0:T, (j % 2) * D:(j % 2 + 1) * D],
                                           normed_t[:, c, j * T:(j + 1) * T], w_o[:, c], start=(c == 0),
                                           stop=(c == CC - 1))
                    mm.then_inc(out_summed, 1)


def after(eng, semaphore, count):
    if not isinstance(count, int) or count > 0:
        eng.wait_ge(semaphore, count)


def every_batch(eng, body):
    for b in (0, 1):
        body(b, b, True)
    with eng.Fori(1, BATCH // 2 - 1) as i:
        for p in range(2):
            body(2 * i + p, p, True)
    for b in (BATCH - 2, BATCH - 1):
        body(b, b % 2, b + 1 < BATCH)


def stage_attention(nc, w, x1):
    with ExitStack() as ctx:
        def sb(name, shape, dt=F32):
            return ctx.enter_context(nc.sbuf_tensor(name, shape, dt))

        def sem(name):
            return ctx.enter_context(nc.semaphore(name))

        w_q = sb("xw_q", [128, CC, D])
        w_k = sb("xw_k", [KC, 2, D])
        w_v = sb("xw_v", [KC, 2, D])
        w_o = sb("xw_o", [128, CC, D])
        b_q = sb("xb_q", [128, CC])
        b_k = sb("xb_k", [128, CC])
        b_v = sb("xb_v", [128, D])
        b_o = sb("xb_o", [T, D])
        ident = sb("xident", [128, 128])
        ident_b = sb("xident_b", [T, T], BF16)
        ones_b = sb("xones_b", [T, 128], BF16)
        power = sb("xpower", [T, 1])
        eps = sb("xeps", [T, 1])
        b_q4 = sb("xb_q4", [128, CC])

        kv = sb("kv", [KC, 2, 2, S])
        stats = sb("xstats", [T, 6])
        mean_var = sb("xmean_var", [T, 2])
        rstd = sb("xrstd", [T, 1])
        xn = sb("xxn", [T, D])
        xn_t = sb("xxn_t", [128, CC, T])
        qf = sb("qf", [128, CC, T])
        qr = sb("qr", [128, CC, T])
        q_part = sb("q_part", [128, 3, CC, T], BF16)
        kf = sb("kf", [128, CC, S])
        kr = sb("kr", [128, CC, S])
        k_part = sb("k_part", [128, 3, CC, S], BF16)
        q_st = sb("q_st", [96, 2, NH, T], BF16)
        k_st = sb("k_st", [96, 2, NH, S], BF16)
        val = sb("xval", [128, 2, 3, NH, 32])
        neg_raw = sb("neg_raw", [T, NH])
        neg_max = sb("neg_max", [T, NH], BF16)
        neg_diag = sb("neg_diag", [T, 2, 4, T], BF16)
        prob = sb("prob", [128, 2, 3, 4 * T])
        mix = sb("mix", [128, T])
        r_den = sb("r_den", [T, NH])
        heads = sb("heads", [T, D])
        heads_t = sb("heads_t", [128, CC, T])
        resid = sb("resid", [T, 2, D])

        bank_s = ctx.enter_context(nc.psum_tensor("bank_s", [128, 2, 512], F32))
        bank_st = [ctx.enter_context(nc.psum_tensor(f"bank_st{i}", [128, 512], F32)) for i in range(3)]
        bank_pv = ctx.enter_context(nc.psum_tensor("bank_pv", [128, 512], F32))
        bank_o = ctx.enter_context(nc.psum_tensor("bank_o", [128, NH, 32], F32))
        bank_m = ctx.enter_context(nc.psum_tensor("bank_m", [128, 512], F32))

        names = ("w_loaded consts waited sp_waited kv_loaded stats_done mv_done eps_added rstd_done xn_done "
                 "xn_turned xn_t_done q_summed q_done q_high q_rest q_mid q_low q_stacked "
                 "k_summed k_done k_high k_rest k_mid k_low k_stacked v_summed v_done "
                 "s_summed max_done neg_done diag_done st_summed clipped shifted exp_done pv_summed "
                 "mix_done o_turned den_done heads_done heads_turned heads_t_done out_summed bias_added "
                 "x_done")
        sems = {n: sem("x_" + n) for n in names.split()}
        (w_loaded, consts, waited, sp_waited, kv_loaded, stats_done, mv_done, eps_added, rstd_done, xn_done,
         xn_turned, xn_t_done, q_summed, q_done, q_high, q_rest, q_mid, q_low, q_stacked,
         k_summed, k_done, k_high, k_rest, k_mid, k_low, k_stacked, v_summed, v_done,
         s_summed, max_done, neg_done, diag_done, st_summed, clipped, shifted, exp_done, pv_summed,
         mix_done, o_turned, den_done, heads_done, heads_turned, heads_t_done, out_summed, bias_added,
         x_done) = sems.values()

        WEIGHTS = [(w_q, w["xq"]), (w_k, w["xk"]), (w_v, w["xv"]), (w_o, w["xo"]), (b_q, w["xbq"]),
                   (b_k, w["xbk"]), (b_v, w["xbv"]), (b_o, w["xbo"]), (ident, w["ident128"])]
        CONSTS = 7
        block = ctx.enter_context(nc.Block())

        @block.sync
        def _(sp):
            def until(semaphore, count):
                if not isinstance(count, int) or count > 0:
                    sp.wait_ge(semaphore, count)
                    sp.sem_inc(sp_waited, 1)

            def load(b, p):
                until(kv_loaded, 16 * b)
                until(v_done, 3 * (b - 1))
                sp.dma_start(kv[:, p], w["ctx_t"][bass.ds(b, 1)].rearrange("o (c p) n -> p (o c) n", c=2)
                             ).then_inc(kv_loaded, 16)

            def stack(b, p):
                def spread(dst, part, slots, parts, c, done):
                    for slot in slots:
                        row = 16 * slot + 8 * c
                        sp.dma_start(dst[row:row + 8, p], part[:, parts, c]).then_inc(done, 16)

                until(st_summed, 12 * (b - 1))
                until(s_summed, 8 * (b - 1))
                for c in range(CC):
                    until(k_high, CC * b + c + 1)
                    spread(k_st, k_part, (0, 2, 5), 0, c, k_stacked)
                    until(k_mid, CC * b + c + 1)
                    spread(k_st, k_part, (1, 4), 1, c, k_stacked)
                    until(k_low, CC * b + c + 1)
                    spread(k_st, k_part, (3,), 2, c, k_stacked)
                until(q_high, b + 1)
                for c in range(CC):
                    spread(q_st, q_part, (0, 1, 3), 0, c, q_stacked)
                until(q_mid, b + 1)
                for c in range(CC):
                    spread(q_st, q_part, (2, 4), 1, c, q_stacked)
                until(q_low, b + 1)
                for c in range(CC):
                    spread(q_st, q_part, (5,), 2, c, q_stacked)

            for tile, src in WEIGHTS:
                sp.dma_start(tile[:], src).then_inc(w_loaded, 16)
            load(0, 0)
            stack(0, 0)

            def body(b, p, more):
                if more:
                    load(b + 1, 1 - p)
                    stack(b + 1, 1 - p)
            every_batch(sp, body)

        @block.gpsimd
        def _(pool):
            pool.memset(power[:], -0.5).then_inc(consts, 1)
            pool.memset(eps[:], EPS).then_inc(consts, 1)
            pool.memset(ones_b[:], 1.0).then_inc(consts, 1)
            pool.memset(val[:], 0.0).then_inc(consts, 1)
            pool.wait_ge(w_loaded, 16 * len(WEIGHTS))
            pool.wait_ge(consts, 4)
            pool.memset(val[:, :, :, :, 16:17], 1.0).then_inc(consts, 1)
            pool.tensor_copy(ident_b[:], ident[0:T, 0:T]).then_inc(consts, 1)
            pool.tensor_scalar(b_q4[:], b_q[:], 0.25, None, ALU.mult).then_inc(consts, 1)
            pool.wait_ge(consts, CONSTS)

            def norm(b):
                pool.wait_ge(mv_done, b + 1)
                pool.tensor_tensor(rstd[:], mean_var[:, 1:2], eps[:], ALU.add).then_inc(eps_added, 1)
                pool.wait_ge(eps_added, b + 1)
                pool.tensor_tensor(rstd[:], rstd[:], power[:], ALU.pow).then_inc(rstd_done, 1)

            def split_k(b, c):
                n = CC * b + c + 1
                pool.wait_ge(k_high, n)
                after(pool, k_stacked, 192 * b)
                pool.tensor_tensor(kr[:, c], kf[:, c], k_part[:, 0, c], ALU.subtract).then_inc(k_rest, 1)
                pool.tensor_tensor(k_part[:, 1, c], kf[:, c], k_part[:, 0, c], ALU.subtract).then_inc(k_mid, 1)
                pool.wait_ge(k_rest, n)
                pool.wait_ge(k_mid, n)
                pool.tensor_tensor(k_part[:, 2, c], kr[:, c], k_part[:, 1, c], ALU.subtract).then_inc(k_low, 1)

            def split_q(b):
                pool.wait_ge(q_high, b + 1)
                after(pool, q_stacked, 192 * b)
                pool.tensor_tensor(qr[:], qf[:], q_part[:, 0], ALU.subtract).then_inc(q_rest, 1)
                pool.tensor_tensor(q_part[:, 1], qf[:], q_part[:, 0], ALU.subtract).then_inc(q_mid, 1)
                pool.wait_ge(q_rest, b + 1)
                pool.wait_ge(q_mid, b + 1)
                pool.tensor_tensor(q_part[:, 2], qr[:], q_part[:, 1], ALU.subtract).then_inc(q_low, 1)

            def diag(b, t):
                n = 4 * b + t
                pool.wait_ge(neg_done, n + 1)
                after(pool, shifted, 3 * (n - 1))
                pool.tensor_tensor(neg_diag[:, t % 2], ident_b[:].unsqueeze(1).to_broadcast([T, 4, T]),
                                   neg_max[:, 4 * t:4 * t + 4].unsqueeze(2).to_broadcast([T, 4, T]),
                                   ALU.mult).then_inc(diag_done, 1)

            norm(0)
            split_k(0, 0)
            split_k(0, 1)
            split_q(0)
            diag(0, 0)

            def body(b, p, more):
                if more:
                    norm(b + 1)
                after(pool, x_done, b - 1)
                pool.tensor_tensor(resid[:, p], x1[:, b, :] if isinstance(b, int) else
                                   x1[:, bass.ds(b, 1), :].rearrange("p o d -> p (o d)"), b_o[:],
                                   ALU.add).then_inc(bias_added, 1)
                if more:
                    split_k(b + 1, 0)
                diag(b, 1)
                if more:
                    split_k(b + 1, 1)
                diag(b, 2)
                if more:
                    split_q(b + 1)
                diag(b, 3)
                if more:
                    diag(b + 1, 0)
            every_batch(pool, body)

        @block.scalar
        def _(act):
            act.wait_ge(consts, CONSTS)

            def keys(b, c):
                n = CC * b + c + 1
                act.wait_ge(k_summed, n)
                after(act, k_low, n - CC)
                act.activation(kf[:, c], bank_m[:, 0:S], ACT.Identity, bias=b_k[:, c:c + 1]).then_inc(k_done, 1)
                act.wait_ge(k_done, n)
                after(act, k_stacked, 192 * b)
                act.activation(k_part[:, 0, c], kf[:, c], ACT.Copy).then_inc(k_high, 1)

            def turned(b):
                act.wait_ge(xn_turned, b + 1)
                act.activation(xn_t[:], bank_m[:, 0:CC * T].rearrange("p (c t) -> p c t", c=CC),
                               ACT.Copy).then_inc(xn_t_done, 1)

            def queries(b):
                act.wait_ge(q_summed, b + 1)
                after(act, q_low, b)
                for c in range(CC):
                    act.activation(qf[:, c], bank_m[:, c * T:(c + 1) * T], ACT.Identity, bias=b_q4[:, c:c + 1],
                                   scale=0.25).then_inc(q_done, 1)
                act.wait_ge(q_done, CC * (b + 1))
                after(act, q_stacked, 192 * b)
                act.activation(q_part[:, 0], qf[:], ACT.Copy).then_inc(q_high, 1)

            def mixed(n):
                after(act, o_turned, n)
                act.wait_ge(pv_summed, n + 1)
                for j in range(4):
                    own = slice(32 * j, 32 * j + 32)
                    act.activation(mix[own], bank_pv[own, j * T:(j + 1) * T], ACT.Copy).then_inc(mix_done, 1)

            def exps(n, t):
                for c in range(3):
                    act.wait_ge(shifted, 3 * n + c + 1)
                    after(act, pv_summed, n - 1)
                    act.activation(prob[0:KEYS[c], t % 2, c], bank_st[c][0:KEYS[c], 0:4 * T],
                                   ACT.Exp).then_inc(exp_done, 1)

            def heads_turn(b):
                act.wait_ge(heads_turned, b + 1)
                act.activation(heads_t[:], bank_m[:, 0:CC * T].rearrange("p (c t) -> p c t", c=CC),
                               ACT.Copy).then_inc(heads_t_done, 1)

            keys(0, 0)
            turned(0)
            keys(0, 1)
            queries(0)

            def body(b, p, more):
                first = isinstance(b, int) and b == 0
                for t in range(4):
                    n = 4 * b + t
                    if not (first and t == 0):
                        mixed(n - 1)
                    exps(n, t)
                    if more and t == 0:
                        keys(b + 1, 0)
                        turned(b + 1)
                    if more and t == 1:
                        keys(b + 1, 1)
                        queries(b + 1)
                    if t == 2 and not first:
                        heads_turn(b - 1)
            every_batch(act, body)
            mixed(4 * BATCH - 1)
            heads_turn(BATCH - 1)

        @block.vector
        def _(dve):
            dve.wait_ge(consts, CONSTS)

            def row(b):
                return x1[:, b, :] if isinstance(b, int) else x1[:, bass.ds(b, 1), :].rearrange("p o d -> p (o d)")

            def norm(b):
                dve.bn_stats(stats[:], row(b)).then_inc(stats_done, 1)
                dve.wait_ge(stats_done, b + 1)
                dve.sem_inc(waited, 1)
                dve.bn_aggr(mean_var[:], stats[:]).then_inc(mv_done, 1)
                dve.wait_ge(rstd_done, b + 1)
                dve.tensor_scalar(xn[:], row(b), mean_var[:, 0:1], rstd[:, 0:1], ALU.subtract,
                                  ALU.mult).then_inc(xn_done, 1)

            def values(b, p, c):
                dve.wait_ge(v_summed, 3 * b + max(c + 1, 2))
                dve.tensor_tensor(val[0:KEYS[c], p, c, :, 0:16],
                                  bank_m[0:KEYS[c], (c % 2) * D:(c % 2 + 1) * D].rearrange("p (h d) -> p h d", d=16),
                                  b_v[0:KEYS[c], :].rearrange("p (h d) -> p h d", d=16),
                                  ALU.add).then_inc(v_done, 1)

            def maxima(n, t, pair):
                dve.wait_ge(s_summed, 2 * n + pair + 1)
                h = 4 * t + 2 * pair
                dve.tensor_reduce(neg_raw[:, h:h + 2], bank_s[0:T, :, 0:S], AX.X, ALU.max,
                                  negate=True).then_inc(max_done, 1)

            def negated(n, t):
                dve.wait_ge(max_done, 2 * n + 2)
                dve.tensor_scalar(neg_max[:, 4 * t:4 * t + 4], neg_raw[:, 4 * t:4 * t + 4], CLAMP, -CLAMP,
                                  ALU.min, ALU.max).then_inc(neg_done, 1)

            def clip(n, c):
                dve.wait_ge(st_summed, 3 * n + c + 1)
                tile = bank_st[c][0:KEYS[c], 0:4 * T]
                dve.tensor_scalar(tile, tile, CLAMP, -CLAMP, ALU.min, ALU.max).then_inc(clipped, 1)

            def normalise(b):
                dve.wait_ge(o_turned, 4 * (b + 1))
                dve.reciprocal(r_den[:], bank_o[0:T, :, 16]).then_inc(den_done, 1)
                dve.wait_ge(den_done, b + 1)
                dve.tensor_tensor(heads[:].rearrange("p (h d) -> p h d", d=16), bank_o[0:T, :, 0:16],
                                  r_den[:].unsqueeze(2).to_broadcast([T, NH, 16]), ALU.mult).then_inc(heads_done, 1)

            def residual(b, p):
                dve.wait_ge(out_summed, b + 1)
                dve.wait_ge(bias_added, b + 1)
                dve.tensor_tensor(row(b), resid[:, p], bank_m[0:T, 0:D], ALU.add).then_inc(x_done, 1)

            norm(0)
            for c in range(3):
                values(0, 0, c)
            maxima(0, 0, 0)
            maxima(0, 0, 1)
            negated(0, 0)

            def body(b, p, more):
                first = isinstance(b, int) and b == 0
                for t in range(4):
                    n = 4 * b + t
                    go = t < 3 or more
                    if go:
                        maxima(n + 1, (t + 1) % 4, 0)
                    if more and t == 0:
                        norm(b + 1)
                    for c in range(3):
                        clip(n, c)
                    if go:
                        maxima(n + 1, (t + 1) % 4, 1)
                        negated(n + 1, (t + 1) % 4)
                    if t == 0 and not first:
                        normalise(b - 1)
                    if t == 2 and not first:
                        residual(b - 1, 1 - p)
                    if t == 3 and more:
                        for c in range(3):
                            values(b + 1, 1 - p, c)
            every_batch(dve, body)
            normalise(BATCH - 1)
            residual(BATCH - 1, (BATCH - 1) % 2)
            dve.wait_ge(x_done, BATCH)

        @block.tensor
        def _(pe):
            pe.wait_ge(w_loaded, 16 * len(WEIGHTS))
            pe.wait_ge(consts, CONSTS)

            def keys(b, p, c):
                if c == 0:
                    pe.wait_ge(kv_loaded, 16 * (b + 1))
                    after(pe, v_done, 3 * b)
                else:
                    pe.wait_ge(xn_t_done, b + 1)
                for i in range(2):
                    mm = pe.matmul(bank_m[:, 0:S], w_k[:, i, c * 128:(c + 1) * 128], kv[:, p, i],
                                   start=(i == 0), stop=(i == 1))
                mm.then_inc(k_summed, 1)

            def turn(b):
                pe.wait_ge(xn_done, b + 1)
                pe.wait_ge(k_done, CC * b + 1)
                for c in range(CC):
                    mm = pe.transpose(bank_m[:, c * T:(c + 1) * T], xn[:, c * 128:(c + 1) * 128], ident[0:T, 0:T])
                mm.then_inc(xn_turned, 1)

            def queries(b):
                pe.wait_ge(k_done, CC * b + 2)
                for m in range(CC):
                    for c in range(CC):
                        mm = pe.matmul(bank_m[:, m * T:(m + 1) * T], w_q[:, c, m * 128:(m + 1) * 128], xn_t[:, c],
                                       start=(c == 0), stop=(c == CC - 1))
                mm.then_inc(q_summed, 1)

            def values(b, p, c):
                if c == 0:
                    pe.wait_ge(q_done, CC * (b + 1))
                    after(pe, x_done, b - 1)
                if c == 2:
                    pe.wait_ge(v_done, 3 * b + 2)
                for i in range(2):
                    mm = pe.matmul(bank_m[0:KEYS[c], (c % 2) * D:(c % 2 + 1) * D],
                                   kv[:, p, i, KEY0[c]:KEY0[c] + KEYS[c]], w_v[:, i], start=(i == 0), stop=(i == 1))
                mm.then_inc(v_summed, 1)

            def scores(b, p, t, pair):
                n = 4 * b + t
                if t == 0 and pair == 0:
                    pe.wait_ge(k_stacked, 192 * (b + 1))
                    pe.wait_ge(q_stacked, 192 * (b + 1))
                after(pe, max_done, 2 * n + pair)
                for i in range(2):
                    h = 4 * t + 2 * pair + i
                    mm = pe.matmul(bank_s[0:T, i, 0:S], q_st[:, p, h], k_st[:, p, h], start=True, stop=True)
                mm.then_inc(s_summed, 1)

            def scores_t(n, p, t, c):
                after(pe, exp_done, 3 * (n - 1) + c + 1)
                for j in range(4):
                    h = 4 * t + j
                    mm = pe.matmul(bank_st[c][0:KEYS[c], j * T:(j + 1) * T],
                                   k_st[:, p, h, KEY0[c]:KEY0[c] + KEYS[c]], q_st[:, p, h], start=(j == 0),
                                   stop=False, skip_group_check=True)
                mm.then_inc(st_summed, 1)

            def shift(n, t, c):
                if c == 0:
                    pe.wait_ge(diag_done, n + 1)
                pe.wait_ge(clipped, 3 * n + c + 1)
                pe.matmul(bank_st[c][0:KEYS[c], 0:4 * T], ones_b[:, 0:KEYS[c]],
                          neg_diag[:, t % 2].rearrange("p j t -> p (j t)"), start=False, stop=True,
                          skip_group_check=True).then_inc(shifted, 1)

            def weigh(n, p, t):
                after(pe, mix_done, 4 * n)
                for c in range(3):
                    pe.wait_ge(exp_done, 3 * n + c + 1)
                    mm = pe.matmul(bank_pv[:, 0:4 * T], val[0:KEYS[c], p, c, 4 * t:4 * t + 4].rearrange("p h d -> p (h d)"),
                                   prob[0:KEYS[c], t % 2, c], start=(c == 0), stop=(c == 2))
                mm.then_inc(pv_summed, 1)

            def turn_heads(b, n, t):
                pe.wait_ge(mix_done, 4 * (n + 1))
                if t == 0:
                    after(pe, heads_done, b)
                pe.transpose(bank_o[0:T, 4 * t:4 * t + 4].rearrange("p h d -> p (h d)"), mix[:],
                             ident[:]).then_inc(o_turned, 1)

            def out_turn(b, reader, count):
                pe.wait_ge(heads_done, b + 1)
                pe.wait_ge(reader, count)
                for c in range(CC):
                    mm = pe.transpose(bank_m[:, c * T:(c + 1) * T], heads[:, c * 128:(c + 1) * 128], ident[0:T, 0:T])
                mm.then_inc(heads_turned, 1)

            def out_project(b):
                pe.wait_ge(heads_t_done, b + 1)
                for c in range(CC):
                    mm = pe.matmul(bank_m[0:T, 0:D], heads_t[:, c], w_o[:, c], start=(c == 0), stop=(c == CC - 1))
                mm.then_inc(out_summed, 1)

            keys(0, 0, 0)
            turn(0)
            keys(0, 0, 1)
            queries(0)
            for c in range(3):
                values(0, 0, c)
            scores(0, 0, 0, 0)
            scores(0, 0, 0, 1)

            def body(b, p, more):
                first = isinstance(b, int) and b == 0
                for t in range(4):
                    n = 4 * b + t
                    nb, np_, nt = (b, p, t + 1) if t < 3 else (b + 1, 1 - p, 0)
                    go = t < 3 or more
                    if go:
                        scores(nb, np_, nt, 0)
                    for c in range(3):
                        scores_t(n, p, t, c)
                    if go:
                        scores(nb, np_, nt, 1)
                    if not (first and t == 0):
                        weigh(n - 1, p if t else 1 - p, (t - 1) % 4)
                    if more and t == 0:
                        keys(b + 1, 1 - p, 0)
                    if more and t == 1:
                        keys(b + 1, 1 - p, 1)
                    if t == 2 and not first:
                        if more:
                            out_turn(b - 1, q_done, CC * (b + 2))
                        else:
                            out_turn(b - 1, v_done, 3 * BATCH)
                    if more and t == 3:
                        values(b + 1, 1 - p, 0)
                        values(b + 1, 1 - p, 1)
                    for c in range(3):
                        shift(n, t, c)
                    if not (first and t == 0):
                        turn_heads(b if t else b - 1, n - 1, (t - 1) % 4)
                    if more and t == 0:
                        turn(b + 1)
                    if more and t == 1:
                        queries(b + 1)
                    if t == 2 and not first:
                        out_project(b - 1)
                    if more and t == 3:
                        values(b + 1, 1 - p, 2)
            every_batch(pe, body)
            weigh(4 * BATCH - 1, (BATCH - 1) % 2, 3)
            turn_heads(BATCH - 1, 4 * BATCH - 1, 3)
            out_turn(BATCH - 1, x_done, BATCH - 1)
            out_project(BATCH - 1)


def stage_routing(nc, w, x1, slots, slot_f, weights, tile_expert, slot_rows):
    with ExitStack() as ctx:
        def sb(name, shape, dt=F32):
            return ctx.enter_context(nc.sbuf_tensor(name, shape, dt))

        def sem(name):
            return ctx.enter_context(nc.semaphore("r_" + name))

        BE = BATCH * E
        w_router = sb("w_router", [128, CC, E])
        ident = sb("rident", [T, T])
        before = sb("before", [T, T])
        ones = sb("rones", [T, T])
        iota_e = sb("iota_e", [T, E])
        iota_full = sb("iota_full", [T, EXPERT_TILES])
        iota_tile = sb("iota_tile", [T, TILES])
        power = sb("rpower", [T, BATCH])
        eps = sb("reps", [T, BATCH])
        stats = sb("rstats", [T, BATCH, 6])
        mean_var = sb("rmean_var", [T, BATCH, 2])
        rstd = sb("rrstd", [T, BATCH])
        xn = sb("rxn", [T, BATCH, D])
        xn_t = sb("rxn_t", [128, 2, CC, T])
        logits = sb("logits", [T, BATCH, E])
        top = sb("top", [T, BATCH, 8])
        index = sb("index", [T, BATCH, 8], U32)
        index_f = sb("index_f", [T, BATCH, 2])
        gap = sb("gap", [T, BATCH])
        gap_exp = sb("gap_exp", [T, BATCH])
        one_hot = sb("one_hot", [T, 2, BATCH, E])
        pairs = sb("pairs", [T, BATCH, E])
        totals = sb("totals", [T, BATCH, E])
        running = sb("running", [T, BATCH, E])
        position = sb("position", [T, BATCH, E])
        needs = sb("needs", [T, E, EXPERT_TILES])
        n_tiles = sb("n_tiles", [T, E])
        end_tile = sb("end_tile", [T, E])
        base = sb("base", [T, E])
        chosen = sb("chosen", [T, 2, BATCH, E])
        past = sb("past", [T, TILES, E])
        expert_f = sb("expert_f", [T, TILES])

        bank_t = [ctx.enter_context(nc.psum_tensor(f"rbank_t{i}", [128, 512], F32)) for i in range(2)]
        bank_l = [ctx.enter_context(nc.psum_tensor(f"rbank_l{i}", [128, 512], F32)) for i in range(2)]
        bank_c = ctx.enter_context(nc.psum_tensor("rbank_c", [128, 512], F32))
        bank_n = ctx.enter_context(nc.psum_tensor("rbank_n", [128, 512], F32))

        w_loaded = sem("w_loaded")
        consts = sem("consts")
        stats_done = sem("stats_done")
        mv_done = sem("mv_done")
        eps_added = sem("eps_added")
        rstd_done = sem("rstd_done")
        xn_done = sem("xn_done")
        turned = sem("turned")
        turned_out = sem("turned_out")
        l_summed = sem("l_summed")
        l_done = sem("l_done")
        exp_done = sem("exp_done")
        pairs_done = sem("pairs_done")
        counted = sem("counted")
        gap_done = sem("gap_done")
        slots_done = sem("slots_done")
        scattered = sem("scattered")
        step = sem("step")

        LOADS = [(w_router, w["router"]), (ident, w["ident"]), (before, w["before"]),
                 (iota_e, w["iota_e"]), (iota_full, w["iota_full"]), (iota_tile, w["iota_tile"])]
        block = ctx.enter_context(nc.Block())

        @block.sync
        def _(sp):
            for tile, src in LOADS:
                sp.dma_start(tile[:], src).then_inc(w_loaded, 16)

        @block.gpsimd
        def _(pool):
            pool.memset(power[:], -0.5).then_inc(consts, 1)
            pool.memset(eps[:], EPS).then_inc(consts, 1)
            pool.memset(ones[:], 1.0).then_inc(consts, 1)
            pool.wait_ge(consts, 3)
            pool.wait_ge(mv_done, BATCH)
            pool.tensor_tensor(rstd[:], mean_var[:, :, 1], eps[:], ALU.add).then_inc(eps_added, 1)
            pool.wait_ge(eps_added, 1)
            pool.tensor_tensor(rstd[:], rstd[:], power[:], ALU.pow).then_inc(rstd_done, 1)
            pool.wait_ge(slots_done, 2)
            pool.wait_ge(xn_done, BATCH)
            for b in range(BATCH):
                for c in range(2):
                    pool.indirect_dma_start(
                        out=slot_rows, out_offset=bass.IndirectOffsetOnAxis(ap=slots[:, c, b:b + 1], axis=0),
                        in_=xn[:, b, :], in_offset=None).then_inc(scattered, 16)
            pool.wait_ge(scattered, 16 * 2 * BATCH)

        @block.scalar
        def _(act):
            act.wait_ge(gap_done, 1)
            act.activation(gap_exp[:], gap[:], ACT.Exp).then_inc(exp_done, 1)

        @block.tensor
        def _(pe):
            pe.wait_ge(w_loaded, 16 * len(LOADS))
            pe.wait_ge(consts, 3)
            for b in range(BATCH + 1):
                if b < BATCH:
                    pe.wait_ge(xn_done, b + 1)
                    if b >= 2:
                        pe.wait_ge(turned_out, b - 1)
                    for c in range(CC):
                        mm = pe.transpose(bank_t[b % 2][:, c * T:(c + 1) * T], xn[:, b, c * 128:(c + 1) * 128],
                                          ident[:])
                    mm.then_inc(turned, 1)
                if b >= 1:
                    o = b - 1
                    pe.wait_ge(turned_out, o + 1)
                    if o >= 2:
                        pe.wait_ge(l_done, o - 1)
                    for c in range(CC):
                        mm = pe.matmul(bank_l[o % 2][0:T, 0:E], xn_t[:, o % 2, c], w_router[:, c],
                                       start=(c == 0), stop=(c == CC - 1))
                    mm.then_inc(l_summed, 1)
            pe.wait_ge(pairs_done, 1)
            flat = pairs[:].rearrange("p b e -> p (b e)")
            pe.matmul(bank_c[0:T, 0:BE], before[:], flat, start=True, stop=True).then_inc(counted, 1)
            pe.matmul(bank_n[0:T, 0:BE], ones[:], flat, start=True, stop=True).then_inc(counted, 1)

        @block.vector
        def _(dve):
            count = [0]

            def then(ins):
                count[0] += 1
                ins.then_inc(step, 1)
                dve.wait_ge(step, count[0])

            for b in range(BATCH):
                dve.bn_stats(stats[:, b], x1[:, b, :]).then_inc(stats_done, 1)
            for b in range(BATCH):
                dve.wait_ge(stats_done, b + 1)
                dve.bn_aggr(mean_var[:, b], stats[:, b]).then_inc(mv_done, 1)
            dve.wait_ge(w_loaded, 16 * len(LOADS))
            dve.wait_ge(rstd_done, 1)
            for b in range(BATCH + 2):
                if b < BATCH:
                    dve.tensor_scalar(xn[:, b], x1[:, b, :], mean_var[:, b, 0:1], rstd[:, b:b + 1],
                                      ALU.subtract, ALU.mult).then_inc(xn_done, 1)
                if 1 <= b <= BATCH:
                    o = b - 1
                    dve.wait_ge(turned, o + 1)
                    if o >= 2:
                        dve.wait_ge(l_summed, o - 1)
                    dve.tensor_copy(xn_t[:, o % 2], bank_t[o % 2][:, 0:CC * T].rearrange("p (c t) -> p c t", c=CC)
                                    ).then_inc(turned_out, 1)
                if b >= 2:
                    o = b - 2
                    dve.wait_ge(l_summed, o + 1)
                    dve.tensor_copy(logits[:, o], bank_l[o % 2][0:T, 0:E]).then_inc(l_done, 1)
                    dve.wait_ge(l_done, o + 1)
                    then(dve.max(top[:, o], logits[:, o]))
                    then(dve.max_index(index[:, o], top[:, o], logits[:, o]))
            dve.tensor_tensor(gap[:], top[:, :, 1], top[:, :, 0], ALU.subtract).then_inc(gap_done, 1)
            then(dve.tensor_copy(index_f[:], index[:, :, 0:2]))
            for c in range(2):
                then(dve.tensor_tensor(one_hot[:, c], index_f[:, :, c:c + 1].to_broadcast([T, BATCH, E]),
                                       iota_e[:].unsqueeze(1).to_broadcast([T, BATCH, E]), ALU.is_equal))
            dve.tensor_tensor(pairs[:], one_hot[:, 0], one_hot[:, 1], ALU.add).then_inc(pairs_done, 1)
            dve.wait_ge(exp_done, 1)
            then(dve.tensor_scalar(gap[:], gap_exp[:], 1.0, None, ALU.add))
            then(dve.reciprocal(weights[:, 0], gap[:]))
            then(dve.tensor_tensor(weights[:, 1], weights[:, 0], gap_exp[:], ALU.mult))
            dve.wait_ge(counted, 2)
            then(dve.tensor_copy(totals[:].rearrange("p b e -> p (b e)"), bank_n[0:T, 0:BE]))
            for e in range(E):
                then(dve.tensor_tensor_scan(running[:, :, e], ones[:, 0:BATCH], totals[:, :, e], 0.0,
                                            ALU.mult, ALU.add))
            then(dve.tensor_tensor(needs[:], running[:, BATCH - 1, :].unsqueeze(2).to_broadcast([T, E, EXPERT_TILES]),
                                   iota_full[:].unsqueeze(1).to_broadcast([T, E, EXPERT_TILES]), ALU.is_gt))
            then(dve.tensor_reduce(n_tiles[:], needs[:], AX.X, ALU.add))
            then(dve.tensor_tensor_scan(end_tile[:], ones[:, 0:E], n_tiles[:], 0.0, ALU.mult, ALU.add))
            then(dve.tensor_tensor(base[:], end_tile[:], n_tiles[:], ALU.subtract))
            then(dve.tensor_scalar(base[:], base[:], 128.0, None, ALU.mult))
            then(dve.tensor_tensor(position[:], running[:], totals[:], ALU.subtract))
            then(dve.tensor_tensor(position[:].rearrange("p b e -> p (b e)"),
                                   position[:].rearrange("p b e -> p (b e)"), bank_c[0:T, 0:BE], ALU.add))
            then(dve.tensor_tensor(position[:], position[:], base[:].unsqueeze(1).to_broadcast([T, BATCH, E]),
                                   ALU.add))
            for c in range(2):
                then(dve.tensor_tensor(chosen[:, c], one_hot[:, c], position[:], ALU.mult))
                then(dve.tensor_reduce(slot_f[:, c], chosen[:, c], AX.X, ALU.add))
                dve.tensor_copy(slots[:, c], slot_f[:, c]).then_inc(slots_done, 1)
            then(dve.tensor_tensor(past[:], iota_tile[:].unsqueeze(2).to_broadcast([T, TILES, E]),
                                   end_tile[:].unsqueeze(1).to_broadcast([T, TILES, E]), ALU.is_ge))
            then(dve.tensor_reduce(expert_f[:], past[:], AX.X, ALU.add))
            then(dve.tensor_scalar(expert_f[:], expert_f[:], float(E - 1), None, ALU.min))
            then(dve.tensor_copy(tile_expert[:], expert_f[0:1, :]))


def stage_experts(nc, w1, w2, ident, tile_expert, slot_rows, slot_out):
    with ExitStack() as ctx:
        def sb(name, shape, dt=F32):
            return ctx.enter_context(nc.sbuf_tensor(name, shape, dt))

        def sem(name):
            return ctx.enter_context(nc.semaphore("e_" + name))

        U = 3
        rows = sb("rows", [128, U, D])
        rows_t = sb("rows_t", [128, U, CC, 128])
        silu = sb("silu", [128, U, F])
        hidden = sb("hidden", [128, U, F])
        hidden_t = sb("hidden_t", [128, U, FC, 128])
        result = sb("result", [128, U, D])
        bank_x = ctx.enter_context(nc.psum_tensor("ebank_x", [128, 512], F32))
        bank_v = [ctx.enter_context(nc.psum_tensor(f"ebank_v{i}", [128, 512], F32)) for i in range(2)]
        bank_g = [ctx.enter_context(nc.psum_tensor(f"ebank_g{i}", [128, 512], F32)) for i in range(2)]
        bank_h = ctx.enter_context(nc.psum_tensor("ebank_h", [128, 512], F32))
        bank_y = ctx.enter_context(nc.psum_tensor("ebank_y", [128, 512], F32))

        loaded = sem("loaded")
        turned = sem("turned")
        rows_t_done = sem("rows_t_done")
        summed = sem("summed")
        silu_done = sem("silu_done")
        hidden_done = sem("hidden_done")
        h_turned = sem("h_turned")
        hidden_t_done = sem("hidden_t_done")
        y_summed = sem("y_summed")
        result_done = sem("result_done")
        stored = sem("stored")
        waited = sem("waited")
        pe_waited = sem("pe_waited")
        pool_waited = sem("pool_waited")
        block = ctx.enter_context(nc.Block())

        def every_tile(eng, body):
            for i in range(6):
                body(i, i % U, i % 2)
            with eng.Fori(1, TILES // 6) as k:
                for i in range(6):
                    body(6 * k + i, i % U, i % 2)
            for i in range(TILES - TILES % 6, TILES):
                body(i, i % U, i % 2)

        @block.sync
        def _(sp):
            def until(semaphore, count):
                if not isinstance(count, int) or count > 0:
                    sp.wait_ge(semaphore, count)
                    sp.sem_inc(waited, 1)

            def body(i, u, bank):
                until(turned, i - 2)
                until(loaded, 16 * i)
                sp.dma_start(rows[:, u], slot_rows[bass.ds(i * 128, 128), :]).then_inc(loaded, 16)
            every_tile(sp, body)

        @block.tensor
        def _(pe):
            def first(i, u, bank):
                pe.wait_ge(loaded, 16 * (i + 1))
                after(pe, rows_t_done, i)
                for c in range(CC):
                    mm = pe.transpose(bank_x[:, c * 128:(c + 1) * 128], rows[:, u, c * 128:(c + 1) * 128], ident[:])
                mm.then_inc(turned, 1)

            def up(i, u, bank):
                expert = pe.value_load(tile_expert[0:1, bass.ds(i, 1)], min_val=0, max_val=E - 1)
                after(pe, hidden_done, i - 1)
                pe.wait_ge(rows_t_done, i + 1)
                pe.sem_inc(pe_waited, 1)
                for half, dst in ((1, bank_g[bank]), (0, bank_v[bank])):
                    for c in range(CC):
                        mm = pe.matmul(dst[:], rows_t[:, u, c], w1[:, bass.ds(expert, 1), c, half * F:(half + 1) * F
                                                                   ].rearrange("p o f -> p (o f)"),
                                       start=(c == 0), stop=(c == CC - 1))
                    mm.then_inc(summed, 1)
                return expert

            def down(i, u, expert):
                pe.wait_ge(hidden_done, i + 1)
                after(pe, hidden_t_done, i)
                for f in range(FC):
                    mm = pe.transpose(bank_h[:, f * 128:(f + 1) * 128], hidden[:, u, f * 128:(f + 1) * 128], ident[:])
                mm.then_inc(h_turned, 1)

            def out(i, u):
                expert = pe.value_load(tile_expert[0:1, bass.ds(i, 1)], min_val=0, max_val=E - 1)
                after(pe, result_done, i)
                pe.wait_ge(hidden_t_done, i + 1)
                pe.sem_inc(pe_waited, 1)
                for f in range(FC):
                    mm = pe.matmul(bank_y[:, 0:D], hidden_t[:, u, f], w2[:, bass.ds(expert, 1), f].rearrange("p o d -> p (o d)"),
                                   start=(f == 0), stop=(f == FC - 1))
                mm.then_inc(y_summed, 1)

            def body(i, u, bank):
                first_tile = isinstance(i, int) and i == 0
                if first_tile:
                    first(0, 0, 0)
                up(i, u, bank)
                if not first_tile:
                    out(i - 1, (u + 2) % U)
                if not (isinstance(i, int) and i == TILES - 1):
                    first(i + 1, (u + 1) % U, 1 - bank)
                down(i, u, None)
            every_tile(pe, body)
            out(TILES - 1, (TILES - 1) % U)

        @block.scalar
        def _(act):
            def body(i, u, bank):
                act.wait_ge(summed, 2 * i + 1)
                after(act, hidden_done, i - 2)
                act.activation(silu[:, u], bank_g[bank][:], ACT.Silu).then_inc(silu_done, 1)
                act.wait_ge(h_turned, i + 1)
                after(act, y_summed, i - 2)
                act.activation(hidden_t[:, u], bank_h[:].rearrange("p (f n) -> p f n", f=FC),
                               ACT.Copy).then_inc(hidden_t_done, 1)
            every_tile(act, body)

        @block.vector
        def _(dve):
            def turn(i, u):
                dve.wait_ge(turned, i + 1)
                after(dve, summed, 2 * (i - 2))
                dve.tensor_copy(rows_t[:, u], bank_x[:, 0:CC * 128].rearrange("p (c n) -> p c n", c=CC)
                                ).then_inc(rows_t_done, 1)

            def result_out(i, u):
                dve.wait_ge(y_summed, i + 1)
                after(dve, stored, 16 * (i - 2))
                dve.tensor_copy(result[:, u], bank_y[:, 0:D]).then_inc(result_done, 1)

            def body(i, u, bank):
                first_tile = isinstance(i, int) and i == 0
                if first_tile:
                    turn(0, 0)
                dve.wait_ge(summed, 2 * i + 2)
                dve.wait_ge(silu_done, i + 1)
                after(dve, h_turned, i - 2)
                dve.tensor_tensor(hidden[:, u], silu[:, u], bank_v[bank][:], ALU.mult).then_inc(hidden_done, 1)
                if not first_tile:
                    result_out(i - 1, (u + 2) % U)
                if not (isinstance(i, int) and i == TILES - 1):
                    turn(i + 1, (u + 1) % U)
            every_tile(dve, body)
            result_out(TILES - 1, (TILES - 1) % U)

        @block.gpsimd
        def _(pool):
            def body(i, u, bank):
                pool.wait_ge(result_done, i + 1)
                after(pool, stored, 16 * i)
                pool.sem_inc(pool_waited, 1)
                pool.dma_start(slot_out[bass.ds(i * 128, 128), :], result[:, u]).then_inc(stored, 16)
            every_tile(pool, body)
            pool.wait_ge(stored, 16 * TILES)


def stage_combine(nc, x1, slots, weights, slot_out, out):
    with ExitStack() as ctx:
        def sem(name):
            return ctx.enter_context(nc.semaphore("c_" + name))

        U = 8
        got = ctx.enter_context(nc.sbuf_tensor("got", [T, U, 2, D], F32))
        gathered = [sem(f"gathered{u}") for u in range(U)]
        half = sem("half")
        summed = sem("summed")
        stored = sem("stored")
        block = ctx.enter_context(nc.Block())

        @block.gpsimd
        def _(pool):
            for b in range(BATCH):
                if b >= U:
                    pool.wait_ge(summed, b - U + 1)
                for c in range(2):
                    pool.indirect_dma_start(
                        out=got[:, b % U, c, :], out_offset=None, in_=slot_out,
                        in_offset=bass.IndirectOffsetOnAxis(ap=slots[:, c, b:b + 1], axis=0)
                    ).then_inc(gathered[b % U], 16)

        @block.vector
        def _(dve):
            for b in range(BATCH):
                dve.wait_ge(gathered[b % U], 32 * (b // U + 1))
                dve.scalar_tensor_tensor(x1[:, b, :], got[:, b % U, 0], weights[:, 0, b:b + 1], x1[:, b, :],
                                         ALU.mult, ALU.add).then_inc(half, 1)
                dve.wait_ge(half, b + 1)
                dve.scalar_tensor_tensor(x1[:, b, :], got[:, b % U, 1], weights[:, 1, b:b + 1], x1[:, b, :],
                                         ALU.mult, ALU.add).then_inc(summed, 1)

        @block.sync
        def _(sp):
            for b in range(0, BATCH, 4):
                sp.wait_ge(summed, b + 4)
                sp.dma_start(out[b:b + 4].rearrange("b t d -> t b d"), x1[:, b:b + 4, :]).then_inc(stored, 16)
            sp.wait_ge(stored, 16 * BATCH // 4)


def decoder_layer(nc, w, out):
    with ExitStack() as ctx:
        def sb(name, shape, dt=F32):
            return ctx.enter_context(nc.sbuf_tensor(name, shape, dt))

        x1 = sb("residual", [T, BATCH, D])
        slots = sb("slots", [T, 2, BATCH], U32)
        slot_f = sb("slot_f", [T, 2, BATCH])
        weights = sb("weights", [T, 2, BATCH])
        tile_expert = sb("tile_expert", [1, TILES], I32)
        zeros = sb("zeros", [128, D])
        slot_rows = nc.dram_tensor("slot_rows", (TILES * 128, D), F32, kind="Internal").ap()
        slot_out = nc.dram_tensor("slot_out", (TILES * 128, D), F32, kind="Internal").ap()
        zeroed = ctx.enter_context(nc.semaphore("zeroed"))
        blank = ctx.enter_context(nc.semaphore("blank"))
        w1_loaded = ctx.enter_context(nc.semaphore("w1_loaded"))
        w2_loaded = ctx.enter_context(nc.semaphore("w2_loaded"))

        with nc.Block() as block:
            @block.gpsimd
            def _(pool):
                pool.memset(zeros[:], 0.0).then_inc(blank, 1)
                pool.wait_ge(blank, 1)
                for i in range(TILES):
                    pool.dma_start(slot_rows[i * 128:(i + 1) * 128, :], zeros[:]).then_inc(zeroed, 16)

        stage_mixer(nc, w, w["x"], x1)
        w1 = sb("expert_w1", [128, E, CC, 2 * F])
        with nc.Block() as block:
            @block.gpsimd
            def _(pool):
                pool.wait_ge(zeroed, 16 * TILES)
                for e in range(E):
                    pool.dma_start(w1[:, e], w["w1"][:, e]).then_inc(w1_loaded, 16)
        stage_attention(nc, w, x1)
        w2 = sb("expert_w2", [128, E, FC, D])
        ident = sb("eident", [128, 128])
        with nc.Block() as block:
            @block.gpsimd
            def _(pool):
                pool.dma_start(ident[:], w["ident128"]).then_inc(w2_loaded, 16)
                for e in range(E):
                    pool.dma_start(w2[:, e], w["w2"][:, e]).then_inc(w2_loaded, 16)
        stage_routing(nc, w, x1, slots, slot_f, weights, tile_expert, slot_rows)
        with nc.Block() as block:
            @block.tensor
            def _(pe):
                pe.wait_ge(w1_loaded, 16 * E)
                pe.wait_ge(w2_loaded, 16 * (E + 1))
        stage_experts(nc, w1, w2, ident, tile_expert, slot_rows, slot_out)
        stage_combine(nc, x1, slots, weights, slot_out, out)


def blocks(a):
    import numpy as np
    return np.ascontiguousarray(a.reshape(-1, 128, a.shape[-1]).transpose(1, 0, 2))


def padded(a, rows, cols):
    import numpy as np
    out = np.zeros((rows, cols), a.dtype)
    out[:a.shape[0], :a.shape[1]] = a
    return out


def level_masks():
    import numpy as np
    s, t = np.arange(T)[:, None], np.arange(T)[None, :]
    out = [s == t]
    for lv in range(1, LEVELS - 1):
        half = 1 << (lv - 1)
        out.append((s // half % 2 == 0) & (t // half == s // half + 1))
    return np.ascontiguousarray(np.stack(out, 1).astype(np.int32))


def laid_out(inputs):
    import numpy as np
    i = {n: np.asarray(a) for n, a in inputs.items()}
    p = {n[8:]: a for n, a in i.items() if n.startswith("L0_attn_")}
    lr = p["W_x1"].shape[0] // BRANCHES
    x2 = np.zeros((128, BRANCHES, D), np.float32)
    for b in range(BRANCHES):
        rows = (b % 4) * lr
        x2[rows:rows + lr, b] = p["W_x2"][:, b * lr:(b + 1) * lr].T
    out = {
        "x": i["x"],
        "x1": blocks(padded(p["W_x1"].T, D, 256)), "x2": x2,
        "r": blocks(p["W_r"].T), "k": blocks(p["W_k"].T), "a": blocks(padded(p["A_w"].T, D, 128)),
        "b": padded(p["B_w"].T, 128, 128), "v": blocks(p["W_v"].T), "g": blocks(p["W_g"].T),
        "o": blocks(p["W_o"].T), "mu_x": p["mu_x"].reshape(CC, 128).T,
        "x_bias": p["x_bias"].reshape(BRANCHES, CC, 128).transpose(2, 0, 1),
        "b_w": p["b_w"].reshape(128, 1), "bonus": p["bonus"].reshape(128, 1),
        "gn_w": np.broadcast_to(p["gn_weight"], (T, 256)), "gn_b": np.broadcast_to(p["gn_bias"], (T, 256)),
        "masks": level_masks(), "ident": np.eye(T, dtype=np.float32),
    }
    a = {n[9:]: v for n, v in i.items() if n.startswith("L0_xattn_")}

    def by_channel(v):
        return v.reshape(*v.shape[:-1], NH, 16).swapaxes(-1, -2).reshape(v.shape)

    def halves(v):
        return v.reshape(2, KC, -1).transpose(1, 0, 2)

    out.update({
        "ctx_t": i["ctx_768"].transpose(0, 2, 1), "xq": blocks(by_channel(a["Wq"])),
        "xk": halves(by_channel(a["Wk"])), "xv": halves(a["Wv"]), "xo": blocks(a["Wo"]),
        "xbq": by_channel(a["bq"]).reshape(CC, 128).T, "xbk": by_channel(a["bk"]).reshape(CC, 128).T,
        "xbv": np.broadcast_to(a["bv"], (128, D)), "xbo": np.broadcast_to(a["bo"], (T, D)),
        "w1": i["L0_ffn_W1"].transpose(2, 0, 1).reshape(CC, 128, E, 2 * F).transpose(1, 2, 0, 3),
        "w2": i["L0_ffn_W2"].transpose(2, 0, 1).reshape(FC, 128, E, D).transpose(1, 2, 0, 3),
        "router": blocks(i["L0_ffn_Wr"].T), "before": np.triu(np.ones((T, T), np.float32), 1),
        "iota_e": np.broadcast_to(np.arange(E, dtype=np.float32), (T, E)),
        "iota_full": np.broadcast_to(128 * np.arange(EXPERT_TILES, dtype=np.float32), (T, EXPERT_TILES)),
        "iota_tile": np.broadcast_to(np.arange(TILES, dtype=np.float32), (T, TILES)),
        "ident128": np.eye(128, dtype=np.float32),
    })
    return {n: np.ascontiguousarray(a) for n, a in out.items()}


def kernel(**inputs):
    import concourse.bacc as bacc
    from concourse.bass_utils import run_bass_kernel_spmd

    nc = bacc.Bacc("TRN2", target_bir_lowering=False, num_devices=1)
    arrays = laid_out(inputs)
    w = {n: nc.dram_tensor(f"in_{n}", a.shape, mybir.dt.from_np(a.dtype), kind="ExternalInput").ap()
         for n, a in arrays.items()}
    out = nc.dram_tensor("out", (BATCH, T, D), F32, kind="ExternalOutput").ap()
    decoder_layer(nc, w, out)
    result = run_bass_kernel_spmd(nc, [{f"in_{n}": a for n, a in arrays.items()}], core_ids=[0])
    return result.results[0]["out"]
```

```python
from contextlib import ExitStack

import concourse.bass as bass
from concourse import mybir

ALU = mybir.AluOpType
ACT = mybir.ActivationFunctionType
AX = mybir.AxisListType
F32 = mybir.dt.float32
BF16 = mybir.dt.bfloat16
U8 = mybir.dt.uint8
U32 = mybir.dt.uint32
I32 = mybir.dt.int32

BATCH, T, D = 32, 100, 256
EPS = 1e-5
G = 4
GROUPS = BATCH // G
GT = G * T
CC = D // 128
RH, RK, RV = 4, 32, 64
TP = 128
BRANCHES = 5
LEVELS = 8
S = 361
KC = 96
NH = 16
KEYS = (121, 120, 120)
KEY0 = (0, 121, 241)
CLAMP = 10000.0
E = 8
F = 512
FC = F // 128
EXPERT_TILES = BATCH * T // 128
TILES = (2 * BATCH * T + E * 127) // 128
ZERO_DMAS = 3
assert TILES % ZERO_DMAS == 0 and E % 2 == 0


def after(eng, semaphore, count):
    if not isinstance(count, int) or count > 0:
        eng.wait_ge(semaphore, count)


def stage_mixer(nc, w, x, x1, zeros, blank, slot_rows, zeroed):
    with ExitStack() as ctx:
        def sb(name, shape, dt=F32):
            return ctx.enter_context(nc.sbuf_tensor(name, shape, dt))

        def sem(name):
            return ctx.enter_context(nc.semaphore(name))

        w_x1 = sb("w_x1", [128, CC, 256])
        w_x2 = sb("w_x2", [128, BRANCHES, 256])
        w_r = sb("w_r", [128, CC, 128])
        w_k = sb("w_k", [128, CC, 128])
        w_a = sb("w_a", [128, CC, 128])
        w_b = sb("w_b", [128, 128])
        w_v = sb("w_v", [128, CC, 256])
        w_g = sb("w_g", [128, CC, 256])
        w_o = sb("w_o", [128, CC, 256])
        mu_x = sb("mu_x", [128, CC])
        mix_bias = sb("mix_bias", [128, BRANCHES, CC])
        b_w = sb("b_w", [128, 1])
        bonus = sb("bonus", [128, 1])
        gn_w = sb("gn_w", [T, 256])
        gn_b = sb("gn_b", [T, 256])
        diagonal = sb("diagonal", [T, T], I32)
        masks = sb("masks", [T, 5, T // 2], I32)
        ident = sb("ident", [T, T])
        power = sb("power", [T, 16])
        eps = sb("eps", [T, 16])

        stats = sb("stats", [T, G, 6])
        mean_var = sb("mean_var", [T, G, 2])
        rstd = sb("rstd", [T, G])
        xn = sb("xn", [T, G, D])
        xn_t = sb("xn_t", [128, CC, G, T + 1])
        delta = sb("delta", [128, CC, G, T])
        xz = sb("xz", [128, CC, G, T])
        z = sb("z", [128, 2, GT])
        part = sb("part", [128, 2, CC, GT])
        mixed = sb("mixed", [128, 2, CC, GT])
        wa = sb("wa", [128, GT])
        rate = sb("rate", [128, GT])
        q = sb("q", [128, 2, G, TP])
        k = sb("k", [128, 2, G, TP])
        decay = sb("decay", [128, 2, G, TP])
        total = sb("total", [128, 2, G * TP // 2])
        q_heads = sb("q_heads", [128, 2, RH, G, T])
        attn = sb("attn", [T, G, RH, T])
        val = sb("val", [T, 2, G, D])
        tanh_g = sb("tanh_g", [T, G, D])
        half_g = sb("half_g", [T, G, D])
        gate = sb("gate", [T, 2, G, D])
        gn_stats = sb("gn_stats", [T, G * RH, 6])
        gn_mv = sb("gn_mv", [T, G * RH, 2])
        gn_rstd = sb("gn_rstd", [T, G * RH])
        normed = sb("normed", [T, G, D])
        normed_t = sb("normed_t", [128, CC, GT])

        bank_f = [ctx.enter_context(nc.psum_tensor(f"bank_f{i}", [128, 512], F32)) for i in range(4)]
        bank_l = [ctx.enter_context(nc.psum_tensor(f"bank_l{i}", [128, 512], F32)) for i in range(2)]
        bank_t = [ctx.enter_context(nc.psum_tensor(f"bank_t{i}", [128, 512], F32)) for i in range(2)]

        x_loaded = sem("x_loaded")
        w_loaded = sem("w_loaded")
        consts = sem("consts")
        waited = sem("waited")
        stats_done = sem("stats_done")
        mv_done = sem("mv_done")
        eps_added = sem("eps_added")
        rstd_done = sem("rstd_done")
        xn_done = sem("xn_done")
        xn_turned = sem("xn_turned")
        xn_t_done = sem("xn_t_done")
        delta_done = sem("delta_done")
        xz_done = sem("xz_done")
        z_summed = sem("z_summed")
        z_done = sem("z_done")
        lora_summed = sem("lora_summed")
        part_done = sem("part_done")
        mixed_done = sem("mixed_done")
        r_summed = sem("r_summed")
        a_summed = sem("a_summed")
        k_summed = sem("k_summed")
        w_summed = sem("w_summed")
        v_summed = sem("v_summed")
        g_summed = sem("g_summed")
        q_done = sem("q_done")
        wa_done = sem("wa_done")
        k_done = sem("k_done")
        rate_done = sem("rate_done")
        decay_done = sem("decay_done")
        val_done = sem("val_done")
        gate_in = sem("gate_in")
        tanh_done = sem("tanh_done")
        gate_done = sem("gate_done")
        q_decayed = sem("q_decayed")
        total_done = sem("total_done")
        k_decayed = sem("k_decayed")
        heads_act = sem("heads_act")
        heads_dve = sem("heads_dve")
        level_summed = sem("level_summed")
        attn_done = sem("attn_done")
        o_summed = sem("o_summed")
        gn_stats_done = sem("gn_stats_done")
        gn_mv_done = sem("gn_mv_done")
        gn_eps = sem("gn_eps")
        gn_rstd_done = sem("gn_rstd_done")
        centred = sem("centred")
        scaled = sem("scaled")
        weighted = sem("weighted")
        shifted = sem("shifted")
        gated = sem("gated")
        o_turned = sem("o_turned")
        normed_t_done = sem("normed_t_done")
        out_summed = sem("out_summed")
        x1_done = sem("x1_done")

        WEIGHTS = [(w_x1, w["x1"]), (w_x2, w["x2"]), (w_r, w["r"]), (w_k, w["k"]), (w_a, w["a"]),
                   (w_b, w["b"]), (w_v, w["v"]), (w_g, w["g"]), (w_o, w["o"]), (mu_x, w["mu_x"]),
                   (mix_bias, w["x_bias"]), (b_w, w["b_w"]), (bonus, w["bonus"]), (gn_w, w["gn_w"]),
                   (gn_b, w["gn_b"]), (masks, w["masks"]), (diagonal, w["diagonal"]), (ident, w["ident"])]
        CONSTS = 10
        LORA_BANK = (0, 1, 2, 3, 1, 2, 0, 1, 3, 0)
        COLS = (T, 50, 50, 48, 48, 48, 64, T - 64)
        COPIES = (4, 2, 2, 2, 2, 2, 4, 2)
        START = tuple(sum(COPIES[:i]) for i in range(LEVELS + 1))

        def odd(tile, lv):
            if lv == LEVELS - 1:
                return tile[:, :, 64:T].unsqueeze(2)
            half = 1 << (lv - 1)
            view = tile.rearrange("p b (s two h) -> p b s two h", two=2, h=half)
            return view[:, :, 0:COLS[lv] // half, 1]

        def every_group(eng, body):
            for g in (0, 1):
                body(g, g, True)
            with eng.Fori(1, GROUPS // 2 - 1) as i:
                for p in range(2):
                    body(2 * i + p, p, True)
            for g in (GROUPS - 2, GROUPS - 1):
                body(g, g % 2, g + 1 < GROUPS)

        def two_more(g):
            return not isinstance(g, int) or g + 2 < GROUPS

        block = ctx.enter_context(nc.Block())

        @block.sync
        def _(sp):
            for g in range(GROUPS):
                if g:
                    sp.wait_ge(x_loaded, 16 * g)
                sp.dma_start(x1[:, g * G:(g + 1) * G, :],
                             x[g * G:(g + 1) * G].rearrange("b t d -> t b d")).then_inc(x_loaded, 16)
                if g == 0:
                    for tile, src in WEIGHTS:
                        sp.dma_start(tile[:], src).then_inc(w_loaded, 16)
            sp.wait_ge(blank, 1)
            n = TILES // ZERO_DMAS
            for i in range(ZERO_DMAS):
                sp.dma_start(slot_rows[i * n * 128:(i + 1) * n * 128, :].rearrange("(n p) d -> p n d", p=128),
                             zeros[:].unsqueeze(1).to_broadcast([128, n, D])).then_inc(zeroed, 16)

        @block.gpsimd
        def _(pool):
            pool.memset(zeros[:], 0.0).then_inc(blank, 1)
            pool.memset(power[:], -0.5).then_inc(consts, 1)
            pool.memset(eps[:], EPS).then_inc(consts, 1)
            pool.memset(xn_t[:, :, :, 0:1], 0.0).then_inc(consts, 1)
            pool.memset(q[:], 0.0).then_inc(consts, 1)
            pool.memset(k[:], 0.0).then_inc(consts, 1)
            pool.memset(decay[:], 1.0).then_inc(consts, 1)
            pool.memset(q_heads[:, 0], 0.0).then_inc(consts, 1)
            pool.memset(q_heads[:, 1], 0.0).then_inc(consts, 1)
            pool.memset(attn[:], 0.0).then_inc(consts, 1)
            pool.memset(total[:], 1.0).then_inc(consts, 1)
            pool.wait_ge(consts, CONSTS)

            def norm(g):
                pool.wait_ge(mv_done, (g + 1) * G)
                pool.tensor_tensor(rstd[:], mean_var[:, :, 1], eps[:, 0:G], ALU.add).then_inc(eps_added, 1)
                pool.wait_ge(eps_added, g + 1)
                pool.tensor_tensor(rstd[:], rstd[:], power[:, 0:G], ALU.pow).then_inc(rstd_done, 1)

            def mix(g, i):
                for c in range(CC):
                    pool.wait_ge(part_done, g * BRANCHES * CC + i * CC + c + 1)
                    after(pool, (g_summed, v_summed, r_summed, a_summed, k_summed)[i] if i > 1 else
                          (v_summed, g_summed)[i], (g + 1) if i > 1 else 2 * g)
                    pool.tensor_tensor(mixed[:, i % 2, c].rearrange("p (b t) -> p b t", b=G),
                                       part[:, i % 2, c].rearrange("p (b t) -> p b t", b=G),
                                       xn_t[:, c, :, 1:T + 1], ALU.add).then_inc(mixed_done, 1)

            def head_norm(g):
                pool.wait_ge(gn_mv_done, (g + 1) * G * RH)
                pool.tensor_tensor(gn_rstd[:], gn_mv[:, :, 1], eps[:], ALU.add).then_inc(gn_eps, 1)
                pool.wait_ge(gn_eps, g + 1)
                pool.tensor_tensor(gn_rstd[:], gn_rstd[:], power[:], ALU.pow).then_inc(gn_rstd_done, 1)

            def finish(g, p, j):
                pool.wait_ge(scaled, g * 2 + j // 2 + 1)
                pool.wait_ge(gate_done, (g + 1) * 2)
                pool.tensor_tensor(normed[:, j], normed[:, j], gn_w[:], ALU.mult).then_inc(weighted, 1)
                pool.wait_ge(weighted, g * G + j + 1)
                pool.tensor_tensor(normed[:, j], normed[:, j], gn_b[:], ALU.add).then_inc(shifted, 1)
                pool.wait_ge(shifted, g * G + j + 1)
                pool.tensor_tensor(normed[:, j], normed[:, j], gate[:, p, j], ALU.mult).then_inc(gated, 1)

            norm(0)
            for i in range(BRANCHES):
                mix(0, i)
            norm(1)

            def body(g, p, more):
                first = isinstance(g, int) and g == 0
                if not first:
                    head_norm(g - 1)
                    finish(g - 1, 1 - p, 0)
                if more:
                    mix(g + 1, 0)
                    mix(g + 1, 1)
                if not first:
                    finish(g - 1, 1 - p, 1)
                if more:
                    mix(g + 1, 2)
                if not first:
                    finish(g - 1, 1 - p, 2)
                if more:
                    mix(g + 1, 3)
                if not first:
                    finish(g - 1, 1 - p, 3)
                if two_more(g):
                    norm(g + 2)
                if more:
                    mix(g + 1, 4)
            every_group(pool, body)
            head_norm(GROUPS - 1)
            for j in range(G):
                finish(GROUPS - 1, (GROUPS - 1) % 2, j)

        @block.scalar
        def _(act):
            act.wait_ge(consts, CONSTS)
            act.wait_ge(w_loaded, 16 * len(WEIGHTS))

            def by_batch(tile):
                return tile.rearrange("p (b t) -> p b t", b=G)

            def front(g, p, piece):
                if piece == 0:
                    for c in range(CC):
                        act.wait_ge(xn_turned, g * CC + c + 1)
                        after(act, mixed_done, g * BRANCHES * CC)
                        after(act, xz_done, g * CC)
                        act.activation(xn_t[:, c, :, 1:T + 1], by_batch(bank_f[c][:, 0:GT]),
                                       ACT.Copy).then_inc(xn_t_done, 1)
                if piece == 1:
                    for m in range(2):
                        act.wait_ge(z_summed, g * 2 + m + 1)
                        after(act, lora_summed, g * BRANCHES * CC)
                        act.activation(z[:, m], bank_f[2 + m][:, 0:GT], ACT.Tanh).then_inc(z_done, 1)
                if piece == 3:
                    act.wait_ge(r_summed, g + 1)
                    after(act, heads_act, 3 * LEVELS * (g - 1))
                    after(act, heads_dve, LEVELS * (g - 1))
                    act.activation(q[:, p, :, 0:T], by_batch(bank_f[0][:, 0:GT]), ACT.Copy).then_inc(q_done, 1)
                if piece == 4:
                    act.wait_ge(a_summed, g + 1)
                    after(act, w_summed, g)
                    act.activation(wa[:], bank_f[3][:, 0:GT], ACT.Tanh).then_inc(wa_done, 1)
                if piece == 5:
                    act.wait_ge(k_summed, g + 1)
                    after(act, level_summed, G * LEVELS * (g - 1))
                    act.activation(k[:, p, :, 0:T], by_batch(bank_f[2][:, 0:GT]), ACT.Copy).then_inc(k_done, 1)
                if piece == 6:
                    act.wait_ge(w_summed, g + 1)
                    act.activation(rate[:], bank_f[1][:, 0:GT], ACT.Exp, bias=b_w[:, 0:1]).then_inc(rate_done, 1)
                    act.wait_ge(rate_done, g + 1)
                    after(act, k_decayed, (LEVELS - 2) * (g - 1))
                    act.activation(decay[:, p, :, 0:T], by_batch(rate[:]), ACT.Exp,
                                   scale=-1.0).then_inc(decay_done, 1)
                    for i in range(2):
                        act.wait_ge(v_summed, g * 2 + i + 1)
                        after(act, o_summed, 2 * (g - 1))
                        act.activation(val[:, p, 2 * i:2 * i + 2],
                                       bank_f[2 + i][0:T].rearrange("p (b d) -> p b d", b=2),
                                       ACT.Copy).then_inc(val_done, 1)
                if piece == 7:
                    for i in range(2):
                        act.wait_ge(g_summed, g * 2 + i + 1)
                        after(act, gate_done, 2 * g)
                        src = bank_f[i][0:T].rearrange("p (b d) -> p b d", b=2)
                        act.activation(tanh_g[:, 2 * i:2 * i + 2], src, ACT.Tanh, scale=0.5).then_inc(tanh_done, 1)
                        act.activation(half_g[:, 2 * i:2 * i + 2], src, ACT.Copy, scale=0.5).then_inc(gate_in, 1)

            def heads(g, p, lv):
                if lv == 0:
                    act.wait_ge(q_done, g + 1)
                if lv >= 2:
                    act.wait_ge(q_decayed, g * (LEVELS - 2) + lv - 1)
                after(act, level_summed, G * (LEVELS * g + lv - 1))
                for h in range(3):
                    rows = slice(RK * h, RK * h + RK)
                    if lv == 0:
                        src, dst = q[rows, p, :, 0:T], q_heads[rows, 0, h]
                    else:
                        src = odd(q[rows, p], lv)
                        dst = q_heads[rows, lv % 2, h, :, 0:COLS[lv]].rearrange(
                            "p b (s h) -> p b s h", s=src.shape[2])
                    act.activation(dst, src, ACT.Copy,
                                   scale=bonus[rows, 0:1] if lv == 0 else 1.0).then_inc(heads_act, 1)

            for piece in range(8):
                front(0, 0, piece)
            heads(0, 0, 0)

            def turned(g):
                for c in range(CC):
                    act.wait_ge(o_turned, g * CC + c + 1)
                    act.activation(normed_t[:, c], bank_t[c][:, 0:GT], ACT.Copy).then_inc(normed_t_done, 1)

            def body(g, p, more):
                first = isinstance(g, int) and g == 0
                for s in range(LEVELS):
                    if s + 1 < LEVELS:
                        heads(g, p, s + 1)
                    elif more:
                        heads(g + 1, 1 - p, 0)
                    if s == 6 and not first:
                        turned(g - 1)
                    if more:
                        front(g + 1, 1 - p, s)
            every_group(act, body)
            turned(GROUPS - 1)

        @block.vector
        def _(dve):
            dve.wait_ge(consts, CONSTS)
            dve.wait_ge(w_loaded, 16 * len(WEIGHTS))

            def rows_of(g, j, n):
                if isinstance(g, int):
                    return x1[:, g * G + j:g * G + j + n, :].rearrange("p b d -> p (b d)")
                return x1[:, bass.ds(g * G + j, n), :].rearrange("p b d -> p (b d)")

            def delta_times(g, i):
                for c in range(CC):
                    n = i * CC + c
                    dve.wait_ge(lora_summed, g * BRANCHES * CC + n + 1)
                    after(dve, mixed_done, g * BRANCHES * CC + n - 2 * CC + 1)
                    dve.scalar_tensor_tensor(part[:, i % 2, c], bank_f[LORA_BANK[n]][:, 0:GT],
                                             mix_bias[:, i, c:c + 1],
                                             delta[:, c].rearrange("p b t -> p (b t)"),
                                             ALU.add, ALU.mult).then_inc(part_done, 1)

            def norm_stats(g):
                dve.wait_ge(x_loaded, (g + 1) * 16)
                for j in range(G):
                    dve.bn_stats(stats[:, j], rows_of(g, j, 1)).then_inc(stats_done, 1)
                dve.wait_ge(stats_done, (g + 1) * G)
                dve.sem_inc(waited, 1)
                for j in range(G):
                    dve.bn_aggr(mean_var[:, j], stats[:, j]).then_inc(mv_done, 1)

            def norm_apply(g):
                dve.wait_ge(rstd_done, g + 1)
                after(dve, xn_turned, g * CC)
                for j in range(G):
                    dve.tensor_scalar(xn[:, j], rows_of(g, j, 1), mean_var[:, j, 0:1], rstd[:, j:j + 1],
                                      ALU.subtract, ALU.mult).then_inc(xn_done, 1)

            def front(g, p, piece):
                if piece == 1:
                    dve.wait_ge(xn_t_done, (g + 1) * CC)
                    dve.tensor_tensor(delta[:].rearrange("p c b t -> p (c b) t"),
                                      xn_t[:, :, :, 0:T].rearrange("p c b t -> p (c b) t"),
                                      xn_t[:, :, :, 1:T + 1].rearrange("p c b t -> p (c b) t"),
                                      ALU.subtract).then_inc(delta_done, 1)
                    dve.wait_ge(delta_done, g + 1)
                    for c in range(CC):
                        dve.scalar_tensor_tensor(xz[:, c], delta[:, c], mu_x[:, c:c + 1],
                                                 xn_t[:, c, :, 1:T + 1], ALU.mult, ALU.add).then_inc(xz_done, 1)
                if piece == 2:
                    delta_times(g, 0)
                    delta_times(g, 1)
                if 3 <= piece <= 5:
                    delta_times(g, piece - 1)
                if piece == 7:
                    for i in range(2):
                        dve.wait_ge(gate_in, g * 2 + i + 1)
                        dve.wait_ge(tanh_done, g * 2 + i + 1)
                        after(dve, gated, G * (g - 1))
                        dve.scalar_tensor_tensor(gate[:, p, 2 * i:2 * i + 2], tanh_g[:, 2 * i:2 * i + 2], 1.0,
                                                 half_g[:, 2 * i:2 * i + 2], ALU.add,
                                                 ALU.mult).then_inc(gate_done, 1)

            def heads(g, p, lv):
                rows = slice(RK * 3, RK * 4)
                if lv == 0:
                    dve.wait_ge(q_done, g + 1)
                if lv >= 2:
                    dve.wait_ge(q_decayed, g * (LEVELS - 2) + lv - 1)
                after(dve, level_summed, G * (LEVELS * g + lv - 1))
                if lv == 0:
                    dve.tensor_scalar(q_heads[rows, 0, 3], q[rows, p, :, 0:T], bonus[rows, 0:1], None,
                                      ALU.mult).then_inc(heads_dve, 1)
                else:
                    src = odd(q[rows, p], lv)
                    dst = q_heads[rows, lv % 2, 3, :, 0:COLS[lv]].rearrange("p b (s h) -> p b s h", s=src.shape[2])
                    dve.tensor_copy(dst, src).then_inc(heads_dve, 1)

            def seg_views(p, lv):
                half = 1 << (lv - 2)
                nseg = G * TP // (2 * half)
                seg = "p (s two h) -> p s two h"
                qv = q[:, p].rearrange("p b t -> p (b t)").rearrange(seg, two=2, h=half)
                kv = k[:, p].rearrange("p b t -> p (b t)").rearrange(seg, two=2, h=half)
                tot = decay[:, p].rearrange("p b t -> p (b t)") if half == 1 else total[:, lv % 2, 0:2 * nseg]
                return half, nseg, qv, kv, tot.rearrange("p (s two) -> p s two", two=2)

            def decay_q(g, p, lv):
                half, nseg, qv, kv, tv = seg_views(p, lv)
                if half == 1:
                    dve.wait_ge(decay_done, g + 1)
                    dve.wait_ge(k_done, g + 1)
                else:
                    dve.wait_ge(total_done, g * (LEVELS - 2) + lv - 2)
                dve.wait_ge(heads_act, 3 * (g * LEVELS + lv))
                dve.wait_ge(heads_dve, g * LEVELS + lv)
                dve.tensor_tensor(qv[:, :, 1], qv[:, :, 1], tv[:, :, 0:1].to_broadcast([128, nseg, half]),
                                  ALU.mult).then_inc(q_decayed, 1)
                after(dve, k_decayed, g * (LEVELS - 2) + lv - 2)
                dve.tensor_tensor(total[:, (lv + 1) % 2, 0:nseg], tv[:, :, 0], tv[:, :, 1],
                                  ALU.mult).then_inc(total_done, 1)

            def decay_k(g, p, lv):
                half, nseg, qv, kv, tv = seg_views(p, lv)
                dve.wait_ge(level_summed, (g * LEVELS + lv) * G)
                dve.tensor_tensor(kv[:, :, 0], kv[:, :, 0], tv[:, :, 1:2].to_broadcast([128, nseg, half]),
                                  ALU.mult).then_inc(k_decayed, 1)

            def collect(g, lv):
                if lv == 0:
                    for j in range(G):
                        dve.wait_ge(level_summed, g * LEVELS * G + j + 1)
                        after(dve, o_summed, 2 * g)
                        dve.sem_inc(waited, 1)
                        dve.copy_predicated(attn[:, j], diagonal[:].unsqueeze(1).to_broadcast([T, RH, T]),
                                            bank_l[j % 2][0:T, 0:GT].rearrange("p (h t) -> p h t", h=RH)
                                            ).then_inc(attn_done, 1)
                    return
                for i in range(2):
                    dve.wait_ge(level_summed, (g * LEVELS + lv) * G + 2 * i + 2)
                    cols = COLS[lv]
                    src = bank_l[i][0:T, 0:8 * cols].rearrange("p (n c) -> p n c", n=8)
                    dst = attn[:, 2 * i:2 * i + 2].rearrange("p b h t -> p (b h) t")
                    if lv == LEVELS - 1:
                        dve.tensor_copy(dst[0:64, :, 64:T], src[0:64]).then_inc(attn_done, 1)
                    elif lv == LEVELS - 2:
                        dve.tensor_copy(dst[0:32, :, 32:64], src[0:32, :, 0:32]).then_inc(attn_done, 1)
                        dve.tensor_copy(dst[64:96, :, 96:T], src[64:96, :, 32:36]).then_inc(attn_done, 1)
                    else:
                        half = 1 << (lv - 1)
                        nseg = cols // half
                        to = dst[:, :, 0:nseg * 2 * half].rearrange("p n (s two h) -> p n s two h", two=2, h=half)
                        mask = masks[:, lv - 1, 0:cols].rearrange("p (s h) -> p s h", h=half)
                        dve.sem_inc(waited, 1)
                        dve.copy_predicated(to[:, :, :, 1], mask.unsqueeze(1).to_broadcast([T, 8, nseg, half]),
                                            src.rearrange("p n (s h) -> p n s h", h=half)).then_inc(attn_done, 1)

            def head_stats(g, bank):
                for n in range(8 * bank, 8 * bank + 8):
                    dve.wait_ge(o_summed, g * 2 + n // 8 + 1)
                    dve.bn_stats(gn_stats[:, n], bank_t[n // 8][0:T, (n % 8) * RV:(n % 8 + 1) * RV]
                                 ).then_inc(gn_stats_done, 1)

            def head_moments(g):
                dve.wait_ge(gn_stats_done, (g + 1) * G * RH)
                dve.sem_inc(waited, 1)
                for n in range(G * RH):
                    dve.bn_aggr(gn_mv[:, n], gn_stats[:, n]).then_inc(gn_mv_done, 1)

            def head_scale(g):
                dve.wait_ge(gn_mv_done, (g + 1) * G * RH)
                after(dve, o_turned, 2 * g)
                for i in range(2):
                    out = normed[:, 2 * i:2 * i + 2].rearrange("p b (h v) -> p (b h) v", h=RH)
                    dve.tensor_tensor(out, bank_t[i][0:T].rearrange("p (n v) -> p n v", v=RV),
                                      gn_mv[:, 8 * i:8 * i + 8, 0:1].to_broadcast([T, 8, RV]),
                                      ALU.subtract).then_inc(centred, 1)
                dve.wait_ge(gn_rstd_done, g + 1)
                for i in range(2):
                    out = normed[:, 2 * i:2 * i + 2].rearrange("p b (h v) -> p (b h) v", h=RH)
                    dve.wait_ge(centred, g * 2 + i + 1)
                    dve.tensor_tensor(out, out, gn_rstd[:, 8 * i:8 * i + 8].unsqueeze(2).to_broadcast([T, 8, RV]),
                                      ALU.mult).then_inc(scaled, 1)

            def residual(g):
                for i in range(2):
                    dve.wait_ge(out_summed, g * 2 + i + 1)
                    res = rows_of(g, 2 * i, 2)
                    dve.tensor_tensor(res, res, bank_t[i][0:T], ALU.add).then_inc(x1_done, 1)

            norm_stats(0)
            norm_apply(0)
            for piece in range(8):
                front(0, 0, piece)
            norm_stats(1)
            norm_apply(1)
            heads(0, 0, 0)

            def body(g, p, more):
                first = isinstance(g, int) and g == 0
                for s in range(LEVELS):
                    if s == 0 and more:
                        front(g + 1, 1 - p, 1)
                    if s == 5 and two_more(g):
                        norm_stats(g + 2)
                    if s + 1 < LEVELS:
                        if s >= 1:
                            decay_q(g, p, s + 1)
                        heads(g, p, s + 1)
                        if s >= 1:
                            decay_k(g, p, s + 1)
                    elif more:
                        heads(g + 1, 1 - p, 0)
                    if s == 0 and not first:
                        head_stats(g - 1, 0)
                    collect(g, s)
                    if s == 0 and not first:
                        head_stats(g - 1, 1)
                        head_moments(g - 1)
                    if s == 1 and not first:
                        head_scale(g - 1)
                    if s == 7 and two_more(g):
                        norm_apply(g + 2)
                    if s == 7 and not first:
                        residual(g - 1)
                    if more and s > 1:
                        front(g + 1, 1 - p, s)
            every_group(dve, body)
            head_stats(GROUPS - 1, 0)
            head_stats(GROUPS - 1, 1)
            head_moments(GROUPS - 1)
            head_scale(GROUPS - 1)
            residual(GROUPS - 1)

        @block.tensor
        def _(pe):
            pe.wait_ge(w_loaded, 16 * len(WEIGHTS))
            pe.wait_ge(consts, CONSTS)

            def project(bank, weight, slot, done):
                for c in range(CC):
                    mm = pe.matmul(bank[:, 0:GT], weight[:, c], mixed[:, slot, c], start=(c == 0), stop=(c == CC - 1))
                mm.then_inc(done, 1)

            def project_rows(bank, i, weight, slot, done):
                for j in (2 * i, 2 * i + 1):
                    for c in range(CC):
                        mm = pe.matmul(bank[0:T, (j % 2) * D:(j % 2 + 1) * D], mixed[:, slot, c, j * T:(j + 1) * T],
                                       weight[:, c], start=(c == 0), stop=(c == CC - 1))
                mm.then_inc(done, 1)

            def front(g, piece):
                part0 = g * BRANCHES * CC

                def lora(i, c):
                    n = i * CC + c
                    pe.matmul(bank_f[LORA_BANK[n]][:, 0:GT], w_x2[:, i, c * 128:(c + 1) * 128], z[:, i // 4],
                              start=True, stop=True).then_inc(lora_summed, 1)

                def mixed_ready(i):
                    pe.wait_ge(mixed_done, part0 + (i + 1) * CC)

                if piece == 0:
                    after(pe, gate_in, 2 * g)
                    pe.wait_ge(xn_done, (g + 1) * G)
                    for c in range(CC):
                        for j in range(G):
                            mm = pe.transpose(bank_f[c][:, j * T:(j + 1) * T], xn[:, j, c * 128:(c + 1) * 128],
                                              ident[:])
                        mm.then_inc(xn_turned, 1)
                if piece == 1:
                    after(pe, val_done, 2 * g)
                    pe.wait_ge(xz_done, (g + 1) * CC)
                    for m in range(2):
                        for c in range(CC):
                            mm = pe.matmul(bank_f[2 + m][:, 0:GT], w_x1[:, c, m * 128:(m + 1) * 128],
                                           xz[:, c].rearrange("p b t -> p (b t)"), start=(c == 0),
                                           stop=(c == CC - 1))
                        mm.then_inc(z_summed, 1)
                if piece == 2:
                    pe.wait_ge(z_done, (g + 1) * 2)
                    for n in range(4):
                        lora(n // 2, n % 2)
                if piece == 3:
                    mixed_ready(0)
                    project(bank_f[0], w_r, 0, r_summed)
                    lora(2, 0)
                    pe.wait_ge(part_done, part0 + 3)
                    lora(2, 1)
                if piece == 4:
                    mixed_ready(1)
                    project(bank_f[3], w_a, 1, a_summed)
                    pe.wait_ge(q_done, g + 1)
                    lora(3, 0)
                    pe.wait_ge(part_done, part0 + 5)
                    lora(3, 1)
                if piece == 5:
                    mixed_ready(2)
                    project(bank_f[2], w_k, 0, k_summed)
                    pe.wait_ge(wa_done, g + 1)
                    lora(4, 0)
                    pe.wait_ge(part_done, part0 + 7)
                    lora(4, 1)
                if piece == 6:
                    pe.wait_ge(part_done, part0 + 8)
                    pe.matmul(bank_f[1][:, 0:GT], w_b[:], wa[:], start=True, stop=True).then_inc(w_summed, 1)
                    mixed_ready(3)
                    pe.wait_ge(k_done, g + 1)
                    project_rows(bank_f[2], 0, w_v, 1, v_summed)
                    pe.wait_ge(part_done, part0 + 9)
                    project_rows(bank_f[3], 1, w_v, 1, v_summed)
                if piece == 7:
                    mixed_ready(4)
                    project_rows(bank_f[0], 0, w_g, 0, g_summed)
                    pe.wait_ge(rate_done, g + 1)
                    project_rows(bank_f[1], 1, w_g, 0, g_summed)

            def level(g, p, lv):
                pe.wait_ge(heads_act, 3 * (g * LEVELS + lv + 1))
                pe.wait_ge(heads_dve, g * LEVELS + lv + 1)
                if lv == 0:
                    pe.wait_ge(k_done, g + 1)
                if lv >= 2:
                    pe.wait_ge(k_decayed, g * (LEVELS - 2) + lv - 1)
                copied = g * START[LEVELS]
                for j in range(G):
                    cols = COLS[lv]
                    if lv == 0:
                        bank, at = bank_l[j % 2], 0
                        after(pe, attn_done, copied - 1 + j if j < 2 else copied + j - 1)
                    else:
                        bank, at = bank_l[j // 2], (j % 2) * RH * cols
                        if j % 2 == 0:
                            i = j // 2
                            pe.wait_ge(attn_done, copied + 3 + i if lv == 1 else
                                       copied + START[lv - 1] + (i + 1) * COPIES[lv - 1] // 2)
                    pe.matmul(bank[0:T, at:at + RH * cols], k[:, p, j, 0:T], q_heads[:, lv % 2, :, j, 0:cols],
                              start=True, stop=True).then_inc(level_summed, 1)

            def weigh(g, p):
                pe.wait_ge(attn_done, (g + 1) * START[LEVELS])
                pe.wait_ge(val_done, (g + 1) * 2)
                after(pe, x1_done, 2 * g)
                for i in range(2):
                    for j in (2 * i, 2 * i + 1):
                        for h in range(RH):
                            mm = pe.matmul(bank_t[i][0:T, (j % 2) * D + h * RV:(j % 2) * D + (h + 1) * RV],
                                           attn[:, j, h, :], val[:, p, j, h * RV:(h + 1) * RV], start=True, stop=True)
                    mm.then_inc(o_summed, 1)

            def turn_out(g):
                pe.wait_ge(centred, (g + 1) * 2)
                for c in range(CC):
                    for j in range(G):
                        if c == 0:
                            pe.wait_ge(gated, g * G + j + 1)
                        mm = pe.transpose(bank_t[c][:, j * T:(j + 1) * T], normed[:, j, c * 128:(c + 1) * 128],
                                          ident[:])
                    mm.then_inc(o_turned, 1)

            def project_out(g):
                pe.wait_ge(normed_t_done, (g + 1) * CC)
                for i in range(2):
                    for j in (2 * i, 2 * i + 1):
                        for c in range(CC):
                            mm = pe.matmul(bank_t[i][0:T, (j % 2) * D:(j % 2 + 1) * D],
                                           normed_t[:, c, j * T:(j + 1) * T], w_o[:, c], start=(c == 0),
                                           stop=(c == CC - 1))
                    mm.then_inc(out_summed, 1)

            for piece in range(8):
                front(0, piece)

            def body(g, p, more):
                first = isinstance(g, int) and g == 0
                if more:
                    front(g + 1, 0)
                if not first:
                    weigh(g - 1, 1 - p)
                for s in range(LEVELS):
                    level(g, p, s)
                    if s == 6 and not first:
                        turn_out(g - 1)
                    if s == 7 and not first:
                        project_out(g - 1)
                    if more and s > 0:
                        front(g + 1, s)
            every_group(pe, body)
            weigh(GROUPS - 1, (GROUPS - 1) % 2)
            turn_out(GROUPS - 1)
            project_out(GROUPS - 1)


def every_batch(eng, body):
    for b in (0, 1):
        body(b, b, True, True)
    with eng.Fori(1, BATCH // 2 - 1) as i:
        for p in range(2):
            body(2 * i + p, p, True, True)
    for b in (BATCH - 2, BATCH - 1):
        body(b, b % 2, b + 1 < BATCH, False)


def stage_attention(nc, w, x1, moments_kept, logits, w1, w1_loaded):
    with ExitStack() as ctx:
        def sb(name, shape, dt=F32):
            return ctx.enter_context(nc.sbuf_tensor(name, shape, dt))

        def sem(name):
            return ctx.enter_context(nc.semaphore(name))

        w_q = sb("xw_q", [128, CC, D])
        w_k = sb("xw_k", [KC, 2, D])
        w_v = sb("xw_v", [KC, 2, D])
        w_o = sb("xw_o", [128, CC, D])
        b_q = sb("xb_q", [128, CC])
        b_k = sb("xb_k", [128, CC])
        b_v = sb("xb_v", [128, D])
        b_o = sb("xb_o", [T, D])
        ident = sb("xident", [128, 128])
        ident_b = sb("xident_b", [T, T], BF16)
        ones_b = sb("xones_b", [T, 128], BF16)
        power = sb("xpower", [T, 1])
        eps = sb("xeps", [T, 1])
        w_router = sb("w_router", [128, CC, E])
        b_q4 = sb("xb_q4", [128, CC])

        kv = sb("kv", [KC, 2, 2, S])
        stats = sb("xstats", [T, 6])
        mean_var = sb("xmean_var", [T, 2])
        rstd = sb("xrstd", [T, 1])
        xn = sb("xxn", [T, D])
        xn_t = sb("xxn_t", [128, CC, T])
        qf = sb("qf", [128, CC, T])
        qr = sb("qr", [128, CC, T])
        q_part = sb("q_part", [128, 3, CC, T], BF16)
        kf = sb("kf", [128, CC, S])
        kr = sb("kr", [128, CC, S])
        k_part = sb("k_part", [128, 3, CC, S], BF16)
        q_st = sb("q_st", [96, 2, NH, T], BF16)
        k_st = sb("k_st", [96, 2, NH, S], BF16)
        val = sb("xval", [128, 2, 3, NH, 17])
        neg_raw = sb("neg_raw", [T, NH])
        neg_max = sb("neg_max", [T, NH], BF16)
        neg_diag = sb("neg_diag", [T, 2, 4, T], BF16)
        prob = sb("prob", [128, 2, 3, 4 * T])
        r_den = sb("r_den", [T, NH])
        heads = sb("heads", [T, D])
        heads_t = sb("heads_t", [128, CC, T])
        resid = sb("resid", [T, 2, D])
        stats3 = sb("stats3", [T, 6])
        moment3 = sb("moment3", [T, 3])
        xn3 = sb("xn3", [T, D])
        xn3_t = sb("xn3_t", [128, CC, T])

        bank_s = ctx.enter_context(nc.psum_tensor("bank_s", [128, 2, 512], F32))
        bank_st = [ctx.enter_context(nc.psum_tensor(f"bank_st{i}", [128, 512], F32)) for i in range(3)]
        bank_v = ctx.enter_context(nc.psum_tensor("bank_v", [128, 512], F32))
        bank_o = ctx.enter_context(nc.psum_tensor("bank_o", [128, NH, 17], F32))
        bank_m = ctx.enter_context(nc.psum_tensor("bank_m", [128, 512], F32))

        names = ("w_loaded consts waited sp_waited kv_loaded stats_done mv_done eps_added rstd_done xn_done "
                 "xn_turned xn_t_done q_summed q_done q_high q_rest q_mid q_low q_stacked "
                 "k_summed k_done k_high k_rest k_mid k_low k_stacked v_summed v_done "
                 "s_summed max_done neg_done diag_done st_summed clipped shifted exp_done pv_summed "
                 "den_done heads_done heads_turned heads_t_done out_summed bias_added "
                 "x_done stats3_done mv3_done eps3_added rstd3_done xn3_done kept xn3_turned xn3_t_done l_summed l_done")
        sems = {n: sem("x_" + n) for n in names.split()}
        (w_loaded, consts, waited, sp_waited, kv_loaded, stats_done, mv_done, eps_added, rstd_done, xn_done,
         xn_turned, xn_t_done, q_summed, q_done, q_high, q_rest, q_mid, q_low, q_stacked,
         k_summed, k_done, k_high, k_rest, k_mid, k_low, k_stacked, v_summed, v_done,
         s_summed, max_done, neg_done, diag_done, st_summed, clipped, shifted, exp_done, pv_summed,
         den_done, heads_done, heads_turned, heads_t_done, out_summed, bias_added,
         x_done, stats3_done, mv3_done, eps3_added, rstd3_done, xn3_done, kept, xn3_turned, xn3_t_done, l_summed,
         l_done) = sems.values()

        WEIGHTS = [(w_q, w["xq"]), (w_k, w["xk"]), (w_v, w["xv"]), (w_o, w["xo"]), (b_q, w["xbq"]),
                   (b_k, w["xbk"]), (b_v, w["xbv"]), (b_o, w["xbo"]), (ident, w["ident128"]),
                   (w_router, w["router"])]
        CONSTS = 7
        STACKED = 6 * CC * 16
        block = ctx.enter_context(nc.Block())

        @block.sync
        def _(sp):
            def until(semaphore, count):
                if not isinstance(count, int) or count > 0:
                    sp.wait_ge(semaphore, count)
                    sp.sem_inc(sp_waited, 1)

            def load(b, p):
                until(kv_loaded, 16 * b)
                until(v_done, 3 * (b - 1))
                sp.dma_start(kv[:, p], w["ctx_t"][bass.ds(b, 1)].rearrange("o (c p) n -> p (o c) n", c=2)
                             ).then_inc(kv_loaded, 16)

            def stack(b, p):
                def spread(dst, part, slots, parts, c, done):
                    for slot in slots:
                        row = 16 * slot + 8 * c
                        sp.dma_start(dst[row:row + 8, p], part[:, parts, c]).then_inc(done, 16)

                until(st_summed, 12 * (b - 1))
                until(s_summed, 8 * (b - 1))
                for c in range(CC):
                    until(k_high, CC * b + c + 1)
                    spread(k_st, k_part, (0, 2, 5), 0, c, k_stacked)
                    until(k_mid, CC * b + c + 1)
                    spread(k_st, k_part, (1, 4), 1, c, k_stacked)
                    until(k_low, CC * b + c + 1)
                    spread(k_st, k_part, (3,), 2, c, k_stacked)
                until(q_high, b + 1)
                for c in range(CC):
                    spread(q_st, q_part, (0, 1, 3), 0, c, q_stacked)
                until(q_mid, b + 1)
                for c in range(CC):
                    spread(q_st, q_part, (2, 4), 1, c, q_stacked)
                until(q_low, b + 1)
                for c in range(CC):
                    spread(q_st, q_part, (5,), 2, c, q_stacked)

            for tile, src in WEIGHTS:
                sp.dma_start(tile[:], src).then_inc(w_loaded, 16)
            load(0, 0)
            load(1, 1)
            stack(0, 0)

            def body(b, p, more, more2):
                if more2:
                    load(b + 2, p)
                if more:
                    stack(b + 1, 1 - p)
                if isinstance(b, int) and b < 2:
                    for e in range(b * E // 2, (b + 1) * E // 2):
                        sp.dma_start(w1[:, e], w["w1"][:, e]).then_inc(w1_loaded, 16)
            every_batch(sp, body)

        @block.gpsimd
        def _(pool):
            pool.memset(power[:], -0.5).then_inc(consts, 1)
            pool.memset(eps[:], EPS).then_inc(consts, 1)
            pool.memset(ones_b[:], 1.0).then_inc(consts, 1)
            pool.memset(val[:], 0.0).then_inc(consts, 1)
            pool.wait_ge(w_loaded, 16 * len(WEIGHTS))
            pool.wait_ge(consts, 4)
            pool.memset(val[:, :, :, :, 16:17], 1.0).then_inc(consts, 1)
            pool.tensor_copy(ident_b[:], ident[0:T, 0:T]).then_inc(consts, 1)
            pool.tensor_scalar(b_q4[:], b_q[:], 0.25, None, ALU.mult).then_inc(consts, 1)
            pool.wait_ge(consts, CONSTS)

            def norm(b):
                pool.wait_ge(mv_done, b + 1)
                pool.tensor_tensor(rstd[:], mean_var[:, 1:2], eps[:], ALU.add).then_inc(eps_added, 1)
                pool.wait_ge(eps_added, b + 1)
                pool.tensor_tensor(rstd[:], rstd[:], power[:], ALU.pow).then_inc(rstd_done, 1)

            def norm3(b):
                pool.wait_ge(mv3_done, b + 1)
                pool.tensor_tensor(moment3[:, 2:3], moment3[:, 1:2], eps[:], ALU.add).then_inc(eps3_added, 1)
                pool.wait_ge(eps3_added, b + 1)
                pool.tensor_tensor(moment3[:, 2:3], moment3[:, 2:3], power[:], ALU.pow).then_inc(rstd3_done, 1)

            def split_k(b, c):
                n = CC * b + c + 1
                pool.wait_ge(k_high, n)
                after(pool, k_stacked, STACKED * b)
                pool.tensor_tensor(kr[:, c], kf[:, c], k_part[:, 0, c], ALU.subtract).then_inc(k_rest, 1)
                pool.tensor_tensor(k_part[:, 1, c], kf[:, c], k_part[:, 0, c], ALU.subtract).then_inc(k_mid, 1)
                pool.wait_ge(k_rest, n)
                pool.wait_ge(k_mid, n)
                pool.tensor_tensor(k_part[:, 2, c], kr[:, c], k_part[:, 1, c], ALU.subtract).then_inc(k_low, 1)

            def split_q(b):
                pool.wait_ge(q_high, b + 1)
                after(pool, q_stacked, STACKED * b)
                pool.tensor_tensor(qr[:], qf[:], q_part[:, 0], ALU.subtract).then_inc(q_rest, 1)
                pool.tensor_tensor(q_part[:, 1], qf[:], q_part[:, 0], ALU.subtract).then_inc(q_mid, 1)
                pool.wait_ge(q_rest, b + 1)
                pool.wait_ge(q_mid, b + 1)
                pool.tensor_tensor(q_part[:, 2], qr[:], q_part[:, 1], ALU.subtract).then_inc(q_low, 1)

            def diag(b, t):
                n = 4 * b + t
                pool.wait_ge(neg_done, n + 1)
                after(pool, shifted, 3 * (n - 1))
                pool.tensor_tensor(neg_diag[:, t % 2], ident_b[:].unsqueeze(1).to_broadcast([T, 4, T]),
                                   neg_max[:, 4 * t:4 * t + 4].unsqueeze(2).to_broadcast([T, 4, T]),
                                   ALU.mult).then_inc(diag_done, 1)

            norm(0)
            split_k(0, 0)
            norm(1)
            split_k(0, 1)
            split_q(0)
            split_k(1, 0)
            diag(0, 0)

            def body(b, p, more, more2):
                if more:
                    split_k(b + 1, 1)
                    split_q(b + 1)
                diag(b, 1)
                if more2:
                    norm(b + 2)
                after(pool, x_done, b - 1)
                pool.tensor_tensor(resid[:, p], x1[:, b, :] if isinstance(b, int) else
                                   x1[:, bass.ds(b, 1), :].rearrange("p o d -> p (o d)"), b_o[:],
                                   ALU.add).then_inc(bias_added, 1)
                diag(b, 2)
                diag(b, 3)
                if not (isinstance(b, int) and b == 0):
                    norm3(b - 1)
                if more2:
                    split_k(b + 2, 0)
                if more:
                    diag(b + 1, 0)
            every_batch(pool, body)
            norm3(BATCH - 1)

        @block.scalar
        def _(act):
            act.wait_ge(consts, CONSTS)

            def keys(b, c):
                n = CC * b + c + 1
                act.wait_ge(k_summed, n)
                after(act, k_low, n - CC)
                act.activation(kf[:, c], bank_m[:, 0:S], ACT.Identity, bias=b_k[:, c:c + 1]).then_inc(k_done, 1)

            def keys_high(b, c):
                n = CC * b + c + 1
                act.wait_ge(k_done, n)
                after(act, k_stacked, STACKED * b)
                act.activation(k_part[:, 0, c], kf[:, c], ACT.Copy).then_inc(k_high, 1)

            def turned(b):
                act.wait_ge(xn_turned, b + 1)
                act.activation(xn_t[:], bank_v[:, 0:CC * T].rearrange("p (c t) -> p c t", c=CC),
                               ACT.Copy).then_inc(xn_t_done, 1)

            def queries(b):
                act.wait_ge(q_summed, b + 1)
                after(act, q_low, b)
                for c in range(CC):
                    act.activation(qf[:, c], bank_v[:, c * T:(c + 1) * T], ACT.Identity, bias=b_q4[:, c:c + 1],
                                   scale=0.25).then_inc(q_done, 1)
                act.wait_ge(q_done, CC * (b + 1))
                after(act, q_stacked, STACKED * b)
                act.activation(q_part[:, 0], qf[:], ACT.Copy).then_inc(q_high, 1)

            def exps(n, t):
                for c in range(3):
                    act.wait_ge(shifted, 3 * n + c + 1)
                    after(act, pv_summed, n - 1)
                    act.activation(prob[0:KEYS[c], t % 2, c], bank_st[c][0:KEYS[c], 0:4 * T],
                                   ACT.Exp).then_inc(exp_done, 1)

            def heads_turn(b):
                act.wait_ge(heads_turned, b + 1)
                act.activation(heads_t[:], bank_m[:, 0:CC * T].rearrange("p (c t) -> p c t", c=CC),
                               ACT.Copy).then_inc(heads_t_done, 1)

            def turned3(b):
                act.wait_ge(xn3_turned, b + 1)
                act.activation(xn3_t[:], bank_m[:, 0:CC * T].rearrange("p (c t) -> p c t", c=CC),
                               ACT.Copy).then_inc(xn3_t_done, 1)

            for b in (0, 1):
                keys(b, 0)
                turned(b)
                keys_high(b, 0)
                keys(b, 1)
                keys_high(b, 1)
                queries(b)

            def body(b, p, more, more2):
                first = isinstance(b, int) and b == 0
                for t in range(4):
                    if t == 1 and not first:
                        heads_turn(b - 1)
                    if t == 0 and not (isinstance(b, int) and b < 2):
                        turned3(b - 2)
                    exps(4 * b + t, t)
                    if more2 and t >= 2:
                        keys(b + 2, t - 2)
                    if more2 and t == 2:
                        turned(b + 2)
                    if more2 and t == 3:
                        queries(b + 2)
                    if more2 and t >= 2:
                        keys_high(b + 2, t - 2)
            every_batch(act, body)
            heads_turn(BATCH - 1)
            turned3(BATCH - 2)
            turned3(BATCH - 1)

        @block.vector
        def _(dve):
            dve.wait_ge(consts, CONSTS)

            def row(b):
                return x1[:, b, :] if isinstance(b, int) else x1[:, bass.ds(b, 1), :].rearrange("p o d -> p (o d)")

            def moments(b):
                dve.bn_stats(stats[:], row(b)).then_inc(stats_done, 1)
                dve.wait_ge(stats_done, b + 1)
                dve.sem_inc(waited, 1)
                dve.bn_aggr(mean_var[:], stats[:]).then_inc(mv_done, 1)

            def norm(b):
                dve.wait_ge(rstd_done, b + 1)
                dve.tensor_scalar(xn[:], row(b), mean_var[:, 0:1], rstd[:, 0:1], ALU.subtract,
                                  ALU.mult).then_inc(xn_done, 1)

            def values(b, p, c):
                dve.wait_ge(v_summed, 3 * b + max(c + 1, 2))
                dve.tensor_tensor(val[0:KEYS[c], p, c, :, 0:16],
                                  bank_v[0:KEYS[c], (c % 2) * D:(c % 2 + 1) * D].rearrange("p (h d) -> p h d", d=16),
                                  b_v[0:KEYS[c], :].rearrange("p (h d) -> p h d", d=16),
                                  ALU.add).then_inc(v_done, 1)

            def maxima(n, t, pair):
                dve.wait_ge(s_summed, 2 * n + pair + 1)
                h = 4 * t + 2 * pair
                dve.tensor_reduce(neg_raw[:, h:h + 2], bank_s[0:T, :, 0:S], AX.X, ALU.max,
                                  negate=True).then_inc(max_done, 1)

            def negated(n, t):
                dve.wait_ge(max_done, 2 * n + 2)
                dve.tensor_scalar(neg_max[:, 4 * t:4 * t + 4], neg_raw[:, 4 * t:4 * t + 4], CLAMP, -CLAMP,
                                  ALU.min, ALU.max).then_inc(neg_done, 1)

            def clip(n, c):
                dve.wait_ge(st_summed, 3 * n + c + 1)
                tile = bank_st[c][0:KEYS[c], 0:4 * T]
                dve.tensor_scalar(tile, tile, CLAMP, -CLAMP, ALU.min, ALU.max).then_inc(clipped, 1)

            def normalise(b):
                dve.wait_ge(pv_summed, 4 * (b + 1))
                dve.reciprocal(r_den[:], bank_o[0:T, :, 16]).then_inc(den_done, 1)
                dve.wait_ge(den_done, b + 1)
                dve.tensor_tensor(heads[:].rearrange("p (h d) -> p h d", d=16), bank_o[0:T, :, 0:16],
                                  r_den[:].unsqueeze(2).to_broadcast([T, NH, 16]), ALU.mult).then_inc(heads_done, 1)

            def moments3(b):
                dve.wait_ge(x_done, b + 1)
                after(dve, kept, b)
                dve.sem_inc(waited, 1)
                dve.bn_stats(stats3[:], row(b)).then_inc(stats3_done, 1)
                dve.wait_ge(stats3_done, b + 1)
                dve.sem_inc(waited, 1)
                dve.bn_aggr(moment3[:, 0:2], stats3[:]).then_inc(mv3_done, 1)

            def norm3(b):
                dve.wait_ge(rstd3_done, b + 1)
                dve.tensor_scalar(xn3[:], row(b), moment3[:, 0:1], moment3[:, 2:3], ALU.subtract,
                                  ALU.mult).then_inc(xn3_done, 1)
                dve.tensor_copy(moments_kept[:, bass.ds(b, 1), :].rearrange("p o i -> p (o i)"),
                                moment3[:]).then_inc(kept, 1)

            def logits_out(b):
                dve.wait_ge(l_summed, b + 1)
                dve.tensor_copy(logits[:, b] if isinstance(b, int) else
                                logits[:, bass.ds(b, 1), :].rearrange("p o e -> p (o e)"),
                                bank_m[0:T, 0:E]).then_inc(l_done, 1)

            def residual(b, p):
                dve.wait_ge(out_summed, b + 1)
                dve.wait_ge(bias_added, b + 1)
                dve.tensor_tensor(row(b), resid[:, p], bank_m[0:T, 0:D], ALU.add).then_inc(x_done, 1)

            moments(0)
            norm(0)
            for c in range(3):
                values(0, 0, c)
            moments(1)
            norm(1)
            maxima(0, 0, 0)
            maxima(0, 0, 1)
            negated(0, 0)

            def body(b, p, more, more2):
                first = isinstance(b, int) and b == 0
                for t in range(4):
                    n = 4 * b + t
                    go = t < 3 or more
                    if go:
                        maxima(n + 1, (t + 1) % 4, 0)
                    if t == 1 and not (isinstance(b, int) and b < 2):
                        logits_out(b - 2)
                    if more2 and t == 1:
                        moments(b + 2)
                    if t == 2 and not first:
                        residual(b - 1, 1 - p)
                    if t == 3 and not first:
                        moments3(b - 1)
                    for c in range(3):
                        clip(n, c)
                    if more2 and t == 1:
                        norm(b + 2)
                    if t == 3 and not first:
                        norm3(b - 1)
                    if go:
                        maxima(n + 1, (t + 1) % 4, 1)
                        negated(n + 1, (t + 1) % 4)
                    if t == 0 and not first:
                        normalise(b - 1)
                    if t == 0 and more:
                        values(b + 1, 1 - p, 0)
                        values(b + 1, 1 - p, 1)
                    if t == 1 and more:
                        values(b + 1, 1 - p, 2)
            every_batch(dve, body)
            normalise(BATCH - 1)
            residual(BATCH - 1, (BATCH - 1) % 2)
            moments3(BATCH - 1)
            logits_out(BATCH - 2)
            norm3(BATCH - 1)
            logits_out(BATCH - 1)

        @block.tensor
        def _(pe):
            pe.wait_ge(w_loaded, 16 * len(WEIGHTS))
            pe.wait_ge(consts, CONSTS)

            def keys(b, p, c):
                if c == 0:
                    pe.wait_ge(kv_loaded, 16 * (b + 1))
                    after(pe, x_done, b - 2)
                after(pe, k_done, CC * b + c)
                for i in range(2):
                    mm = pe.matmul(bank_m[:, 0:S], w_k[:, i, c * 128:(c + 1) * 128], kv[:, p, i],
                                   start=(i == 0), stop=(i == 1))
                mm.then_inc(k_summed, 1)

            def turn(b):
                pe.wait_ge(xn_done, b + 1)
                after(pe, v_done, 3 * b)
                for c in range(CC):
                    mm = pe.transpose(bank_v[:, c * T:(c + 1) * T], xn[:, c * 128:(c + 1) * 128], ident[0:T, 0:T])
                mm.then_inc(xn_turned, 1)

            def queries(b):
                pe.wait_ge(xn_t_done, b + 1)
                for m in range(CC):
                    for c in range(CC):
                        mm = pe.matmul(bank_v[:, m * T:(m + 1) * T], w_q[:, c, m * 128:(m + 1) * 128], xn_t[:, c],
                                       start=(c == 0), stop=(c == CC - 1))
                mm.then_inc(q_summed, 1)

            def values(b, p, c):
                if c == 0:
                    pe.wait_ge(q_done, CC * (b + 1))
                if c == 2:
                    pe.wait_ge(v_done, 3 * b + 2)
                for i in range(2):
                    mm = pe.matmul(bank_v[0:KEYS[c], (c % 2) * D:(c % 2 + 1) * D],
                                   kv[:, p, i, KEY0[c]:KEY0[c] + KEYS[c]], w_v[:, i], start=(i == 0), stop=(i == 1))
                mm.then_inc(v_summed, 1)

            def scores(b, p, t, pair):
                n = 4 * b + t
                if t == 0 and pair == 0:
                    pe.wait_ge(k_stacked, STACKED * (b + 1))
                    pe.wait_ge(q_stacked, STACKED * (b + 1))
                after(pe, max_done, 2 * n + pair)
                for i in range(2):
                    h = 4 * t + 2 * pair + i
                    mm = pe.matmul(bank_s[0:T, i, 0:S], q_st[:, p, h], k_st[:, p, h], start=True, stop=True)
                mm.then_inc(s_summed, 1)

            def scores_t(n, p, t, c):
                after(pe, exp_done, 3 * (n - 1) + c + 1)
                for j in range(4):
                    h = 4 * t + j
                    mm = pe.matmul(bank_st[c][0:KEYS[c], j * T:(j + 1) * T],
                                   k_st[:, p, h, KEY0[c]:KEY0[c] + KEYS[c]], q_st[:, p, h], start=(j == 0),
                                   stop=False, skip_group_check=True)
                mm.then_inc(st_summed, 1)

            def shift(n, t, c):
                if c == 0:
                    pe.wait_ge(diag_done, n + 1)
                pe.wait_ge(clipped, 3 * n + c + 1)
                pe.matmul(bank_st[c][0:KEYS[c], 0:4 * T], ones_b[:, 0:KEYS[c]],
                          neg_diag[:, t % 2].rearrange("p j t -> p (j t)"), start=False, stop=True,
                          skip_group_check=True).then_inc(shifted, 1)

            def weigh(b, p, t):
                if t == 0:
                    after(pe, heads_done, b)
                pe.wait_ge(exp_done, 3 * (4 * b + t + 1))
                for j in range(4):
                    for c in range(3):
                        mm = pe.matmul(bank_o[0:T, 4 * t + j], prob[0:KEYS[c], t % 2, c, j * T:(j + 1) * T],
                                       val[0:KEYS[c], p, c, 4 * t + j], start=(c == 0), stop=(c == 2))
                mm.then_inc(pv_summed, 1)

            def out_turn(b, reader, count):
                pe.wait_ge(heads_done, b + 1)
                pe.wait_ge(reader, count)
                for c in range(CC):
                    mm = pe.transpose(bank_m[:, c * T:(c + 1) * T], heads[:, c * 128:(c + 1) * 128], ident[0:T, 0:T])
                mm.then_inc(heads_turned, 1)

            def out_project(b):
                pe.wait_ge(heads_t_done, b + 1)
                for c in range(CC):
                    mm = pe.matmul(bank_m[0:T, 0:D], heads_t[:, c], w_o[:, c], start=(c == 0), stop=(c == CC - 1))
                mm.then_inc(out_summed, 1)

            def turn3(b, reader, count):
                pe.wait_ge(xn3_done, b + 1)
                if reader is not None:
                    pe.wait_ge(reader, count)
                for c in range(CC):
                    mm = pe.transpose(bank_m[:, c * T:(c + 1) * T], xn3[:, c * 128:(c + 1) * 128], ident[0:T, 0:T])
                mm.then_inc(xn3_turned, 1)

            def route(b):
                pe.wait_ge(xn3_t_done, b + 1)
                for c in range(CC):
                    mm = pe.matmul(bank_m[0:T, 0:E], xn3_t[:, c], w_router[:, c], start=(c == 0), stop=(c == CC - 1))
                mm.then_inc(l_summed, 1)

            for b in (0, 1):
                keys(b, b, 0)
                turn(b)
                keys(b, b, 1)
                queries(b)
                if b == 0:
                    for c in range(3):
                        values(0, 0, c)
            scores(0, 0, 0, 0)
            scores(0, 0, 0, 1)

            def body(b, p, more, more2):
                first = isinstance(b, int) and b == 0
                routed = not (isinstance(b, int) and b < 2)
                for t in range(4):
                    n = 4 * b + t
                    nb, np_, nt = (b, p, t + 1) if t < 3 else (b + 1, 1 - p, 0)
                    go = t < 3 or more
                    if go:
                        scores(nb, np_, nt, 0)
                    for c in range(3):
                        scores_t(n, p, t, c)
                    if t == 0 and routed:
                        if more:
                            turn3(b - 2, k_done, CC * (b + 2))
                        else:
                            turn3(b - 2, x_done, BATCH - 2)
                    if not (first and t == 0):
                        weigh(b if t else b - 1, p if t else 1 - p, (t - 1) % 4)
                    if go:
                        scores(nb, np_, nt, 1)
                    if more and t == 0:
                        values(b + 1, 1 - p, 0)
                        values(b + 1, 1 - p, 1)
                    if t == 1 and not first:
                        if routed:
                            out_turn(b - 1, l_done, b - 1)
                        else:
                            out_turn(b - 1, k_done, CC * (b + 2))
                    if more2 and t >= 2:
                        keys(b + 2, p, t - 2)
                    if more and t == 1:
                        values(b + 1, 1 - p, 2)
                    for c in range(3):
                        shift(n, t, c)
                    if t == 0 and routed:
                        route(b - 2)
                    if t == 1 and not first:
                        out_project(b - 1)
                    if more2 and t == 2:
                        turn(b + 2)
                    if more2 and t == 3:
                        queries(b + 2)
            every_batch(pe, body)
            weigh(BATCH - 1, (BATCH - 1) % 2, 3)
            out_turn(BATCH - 1, x_done, BATCH - 1)
            out_project(BATCH - 1)
            turn3(BATCH - 2, x_done, BATCH)
            route(BATCH - 2)
            turn3(BATCH - 1, l_done, BATCH - 1)
            route(BATCH - 1)


def stage_routing(nc, w, x1, moments, logits, slots, slot_f, weights, tile_expert, slot_rows, zeroed, w2, ident128, w2_loaded):
    with ExitStack() as ctx:
        def sb(name, shape, dt=F32):
            return ctx.enter_context(nc.sbuf_tensor(name, shape, dt))

        def sem(name):
            return ctx.enter_context(nc.semaphore("r_" + name))

        BE = BATCH * E
        before = sb("before", [T, T])
        ones = sb("rones", [T, T])
        iota_e = sb("iota_e", [T, E])
        iota_full = sb("iota_full", [T, EXPERT_TILES])
        iota_tile = sb("iota_tile", [T, TILES])
        top = sb("top", [T, BATCH, 8])
        index = sb("index", [T, BATCH, 8], U32)
        xn = sb("rxn", [T, BATCH, D])
        index_f = sb("index_f", [T, BATCH, 2])
        gap = sb("gap", [T, BATCH])
        gap_exp = sb("gap_exp", [T, BATCH])
        one_hot = sb("one_hot", [T, 2, BATCH, E])
        pairs = sb("pairs", [T, BATCH, E])
        totals = sb("totals", [T, BATCH, E])
        running = sb("running", [T, BATCH, E])
        position = sb("position", [T, BATCH, E])
        needs = sb("needs", [T, E, EXPERT_TILES])
        n_tiles = sb("n_tiles", [T, E])
        end_tile = sb("end_tile", [T, E])
        base = sb("base", [T, E])
        chosen = sb("chosen", [T, 2, BATCH, E])
        past = sb("past", [T, TILES, E])
        expert_f = sb("expert_f", [T, TILES])

        bank_c = ctx.enter_context(nc.psum_tensor("rbank_c", [128, 512], F32))
        bank_n = ctx.enter_context(nc.psum_tensor("rbank_n", [128, 512], F32))

        w_loaded = sem("w_loaded")
        consts = sem("consts")
        xn_done = sem("xn_done")
        top_done = sem("top_done")
        index_done = sem("index_done")
        exp_done = sem("exp_done")
        pairs_done = sem("pairs_done")
        counted = sem("counted")
        gap_done = sem("gap_done")
        slots_done = sem("slots_done")
        scattered = sem("scattered")
        step = sem("step")

        LOADS = [(before, w["before"]),
                 (iota_e, w["iota_e"]), (iota_full, w["iota_full"]), (iota_tile, w["iota_tile"])]
        block = ctx.enter_context(nc.Block())

        @block.sync
        def _(sp):
            for tile, src in LOADS:
                sp.dma_start(tile[:], src).then_inc(w_loaded, 16)
            sp.dma_start(ident128[:], w["ident128"]).then_inc(w2_loaded, 16)
            for e in range(E):
                sp.dma_start(w2[:, e], w["w2"][:, e]).then_inc(w2_loaded, 16)

        @block.gpsimd
        def _(pool):
            pool.memset(ones[:], 1.0).then_inc(consts, 1)
            pool.wait_ge(slots_done, 2)
            pool.wait_ge(zeroed, 16 * ZERO_DMAS)
            for b in range(BATCH):
                pool.wait_ge(xn_done, b + 1)
                for c in range(2):
                    pool.indirect_dma_start(
                        out=slot_rows, out_offset=bass.IndirectOffsetOnAxis(ap=slots[:, c, b:b + 1], axis=0),
                        in_=xn[:, b, :], in_offset=None).then_inc(scattered, 16)
            pool.wait_ge(scattered, 16 * 2 * BATCH)

        @block.scalar
        def _(act):
            act.wait_ge(gap_done, 1)
            act.activation(gap_exp[:], gap[:], ACT.Exp).then_inc(exp_done, 1)

        @block.tensor
        def _(pe):
            pe.wait_ge(w_loaded, 16 * len(LOADS))
            pe.wait_ge(consts, 1)
            pe.wait_ge(pairs_done, 1)
            flat = pairs[:].rearrange("p b e -> p (b e)")
            pe.matmul(bank_c[0:T, 0:BE], before[:], flat, start=True, stop=True).then_inc(counted, 1)
            pe.matmul(bank_n[0:T, 0:BE], ones[:], flat, start=True, stop=True).then_inc(counted, 1)

        @block.vector
        def _(dve):
            count = [0]

            def then(ins):
                count[0] += 1
                ins.then_inc(step, 1)
                dve.wait_ge(step, count[0])

            for b in range(BATCH):
                dve.max(top[:, b], logits[:, b]).then_inc(top_done, 1)
            for b in range(BATCH):
                dve.wait_ge(top_done, b + 1)
                dve.max_index(index[:, b], top[:, b], logits[:, b]).then_inc(index_done, 1)
            dve.wait_ge(index_done, BATCH)
            dve.wait_ge(w_loaded, 16 * len(LOADS))
            dve.wait_ge(consts, 1)
            dve.tensor_tensor(gap[:], top[:, :, 1], top[:, :, 0], ALU.subtract).then_inc(gap_done, 1)
            then(dve.tensor_copy(index_f[:], index[:, :, 0:2]))
            for c in range(2):
                then(dve.tensor_tensor(one_hot[:, c], index_f[:, :, c:c + 1].to_broadcast([T, BATCH, E]),
                                       iota_e[:].unsqueeze(1).to_broadcast([T, BATCH, E]), ALU.is_equal))
            dve.tensor_tensor(pairs[:], one_hot[:, 0], one_hot[:, 1], ALU.add).then_inc(pairs_done, 1)
            dve.wait_ge(exp_done, 1)
            then(dve.tensor_scalar(gap[:], gap_exp[:], 1.0, None, ALU.add))
            then(dve.reciprocal(weights[:, 0], gap[:]))
            then(dve.tensor_tensor(weights[:, 1], weights[:, 0], gap_exp[:], ALU.mult))
            dve.wait_ge(counted, 2)
            then(dve.tensor_copy(totals[:].rearrange("p b e -> p (b e)"), bank_n[0:T, 0:BE]))
            for e in range(E):
                then(dve.tensor_tensor_scan(running[:, :, e], ones[:, 0:BATCH], totals[:, :, e], 0.0,
                                            ALU.mult, ALU.add))
            then(dve.tensor_tensor(needs[:], running[:, BATCH - 1, :].unsqueeze(2).to_broadcast([T, E, EXPERT_TILES]),
                                   iota_full[:].unsqueeze(1).to_broadcast([T, E, EXPERT_TILES]), ALU.is_gt))
            then(dve.tensor_reduce(n_tiles[:], needs[:], AX.X, ALU.add))
            then(dve.tensor_tensor_scan(end_tile[:], ones[:, 0:E], n_tiles[:], 0.0, ALU.mult, ALU.add))
            then(dve.tensor_tensor(base[:], end_tile[:], n_tiles[:], ALU.subtract))
            then(dve.tensor_scalar(base[:], base[:], 128.0, None, ALU.mult))
            then(dve.tensor_tensor(position[:], running[:], totals[:], ALU.subtract))
            then(dve.tensor_tensor(position[:].rearrange("p b e -> p (b e)"),
                                   position[:].rearrange("p b e -> p (b e)"), bank_c[0:T, 0:BE], ALU.add))
            then(dve.tensor_tensor(position[:], position[:], base[:].unsqueeze(1).to_broadcast([T, BATCH, E]),
                                   ALU.add))
            for c in range(2):
                then(dve.tensor_tensor(chosen[:, c], one_hot[:, c], position[:], ALU.mult))
                then(dve.tensor_reduce(slot_f[:, c], chosen[:, c], AX.X, ALU.add))
                dve.tensor_copy(slots[:, c], slot_f[:, c]).then_inc(slots_done, 1)
            for b in range(BATCH):
                dve.tensor_scalar(xn[:, b], x1[:, b, :], moments[:, b, 0:1], moments[:, b, 2:3],
                                  ALU.subtract, ALU.mult).then_inc(xn_done, 1)
            then(dve.tensor_tensor(past[:], iota_tile[:].unsqueeze(2).to_broadcast([T, TILES, E]),
                                   end_tile[:].unsqueeze(1).to_broadcast([T, TILES, E]), ALU.is_ge))
            then(dve.tensor_reduce(expert_f[:], past[:], AX.X, ALU.add))
            then(dve.tensor_scalar(expert_f[:], expert_f[:], float(E - 1), None, ALU.min))
            then(dve.tensor_copy(tile_expert[:], expert_f[0:1, :]))


def stage_experts(nc, w1, w1_loaded, w2, ident, w2_loaded, tile_expert, slot_rows, slot_out):
    with ExitStack() as ctx:
        def sb(name, shape, dt=F32):
            return ctx.enter_context(nc.sbuf_tensor(name, shape, dt))

        def sem(name):
            return ctx.enter_context(nc.semaphore("e_" + name))

        U = 3
        rows = sb("rows", [128, U, D])
        rows_t = sb("rows_t", [128, U, CC, 128])
        silu = sb("silu", [128, U, F])
        hidden = sb("hidden", [128, U, F])
        hidden_t = sb("hidden_t", [128, U, FC, 128])
        result = sb("result", [128, U, D])
        bank_x = ctx.enter_context(nc.psum_tensor("ebank_x", [128, 512], F32))
        bank_v = [ctx.enter_context(nc.psum_tensor(f"ebank_v{i}", [128, 512], F32)) for i in range(2)]
        bank_g = [ctx.enter_context(nc.psum_tensor(f"ebank_g{i}", [128, 512], F32)) for i in range(2)]
        bank_h = ctx.enter_context(nc.psum_tensor("ebank_h", [128, 512], F32))
        bank_y = ctx.enter_context(nc.psum_tensor("ebank_y", [128, 512], F32))

        loaded = sem("loaded")
        turned = sem("turned")
        rows_t_done = sem("rows_t_done")
        summed = sem("summed")
        silu_done = sem("silu_done")
        hidden_done = sem("hidden_done")
        h_turned = sem("h_turned")
        hidden_t_done = sem("hidden_t_done")
        y_summed = sem("y_summed")
        result_done = sem("result_done")
        stored = sem("stored")
        waited = sem("waited")
        pe_waited = sem("pe_waited")
        pool_waited = sem("pool_waited")
        block = ctx.enter_context(nc.Block())

        def every_tile(eng, body):
            for i in range(6):
                body(i, i % U, i % 2)
            with eng.Fori(1, TILES // 6) as k:
                for i in range(6):
                    body(6 * k + i, i % U, i % 2)
            for i in range(TILES - TILES % 6, TILES):
                body(i, i % U, i % 2)

        @block.sync
        def _(sp):
            def until(semaphore, count):
                if not isinstance(count, int) or count > 0:
                    sp.wait_ge(semaphore, count)
                    sp.sem_inc(waited, 1)

            def body(i, u, bank):
                until(turned, i - 2)
                until(loaded, 16 * i)
                sp.dma_start(rows[:, u], slot_rows[bass.ds(i * 128, 128), :]).then_inc(loaded, 16)
            every_tile(sp, body)

        @block.tensor
        def _(pe):
            pe.wait_ge(w1_loaded, 16 * E)
            pe.wait_ge(w2_loaded, 16 * (E + 1))

            def first(i, u, bank):
                pe.wait_ge(loaded, 16 * (i + 1))
                after(pe, rows_t_done, i)
                for c in range(CC):
                    mm = pe.transpose(bank_x[:, c * 128:(c + 1) * 128], rows[:, u, c * 128:(c + 1) * 128], ident[:])
                mm.then_inc(turned, 1)

            def up(i, u, bank):
                expert = pe.value_load(tile_expert[0:1, bass.ds(i, 1)], min_val=0, max_val=E - 1)
                after(pe, hidden_done, i - 1)
                pe.wait_ge(rows_t_done, i + 1)
                pe.sem_inc(pe_waited, 1)
                for half, dst in ((1, bank_g[bank]), (0, bank_v[bank])):
                    for c in range(CC):
                        mm = pe.matmul(dst[:], rows_t[:, u, c], w1[:, bass.ds(expert, 1), c, half * F:(half + 1) * F
                                                                   ].rearrange("p o f -> p (o f)"),
                                       start=(c == 0), stop=(c == CC - 1))
                    mm.then_inc(summed, 1)
                return expert

            def down(i, u, expert):
                pe.wait_ge(hidden_done, i + 1)
                after(pe, hidden_t_done, i)
                for f in range(FC):
                    mm = pe.transpose(bank_h[:, f * 128:(f + 1) * 128], hidden[:, u, f * 128:(f + 1) * 128], ident[:])
                mm.then_inc(h_turned, 1)

            def out(i, u):
                expert = pe.value_load(tile_expert[0:1, bass.ds(i, 1)], min_val=0, max_val=E - 1)
                after(pe, result_done, i)
                pe.wait_ge(hidden_t_done, i + 1)
                pe.sem_inc(pe_waited, 1)
                for f in range(FC):
                    mm = pe.matmul(bank_y[:, 0:D], hidden_t[:, u, f], w2[:, bass.ds(expert, 1), f].rearrange("p o d -> p (o d)"),
                                   start=(f == 0), stop=(f == FC - 1))
                mm.then_inc(y_summed, 1)

            def body(i, u, bank):
                first_tile = isinstance(i, int) and i == 0
                if first_tile:
                    first(0, 0, 0)
                up(i, u, bank)
                if not (isinstance(i, int) and i == TILES - 1):
                    first(i + 1, (u + 1) % U, 1 - bank)
                if not first_tile:
                    out(i - 1, (u + 2) % U)
                down(i, u, None)
            every_tile(pe, body)
            out(TILES - 1, (TILES - 1) % U)

        @block.scalar
        def _(act):
            def body(i, u, bank):
                act.wait_ge(summed, 2 * i + 1)
                after(act, hidden_done, i - 2)
                act.activation(silu[:, u], bank_g[bank][:], ACT.Silu).then_inc(silu_done, 1)
                act.wait_ge(h_turned, i + 1)
                after(act, y_summed, i - 2)
                act.activation(hidden_t[:, u], bank_h[:].rearrange("p (f n) -> p f n", f=FC),
                               ACT.Copy).then_inc(hidden_t_done, 1)
            every_tile(act, body)

        @block.vector
        def _(dve):
            def turn(i, u):
                dve.wait_ge(turned, i + 1)
                after(dve, summed, 2 * (i - 2))
                dve.tensor_copy(rows_t[:, u], bank_x[:, 0:CC * 128].rearrange("p (c n) -> p c n", c=CC)
                                ).then_inc(rows_t_done, 1)

            def result_out(i, u):
                dve.wait_ge(y_summed, i + 1)
                after(dve, stored, 16 * (i - 2))
                dve.tensor_copy(result[:, u], bank_y[:, 0:D]).then_inc(result_done, 1)

            def body(i, u, bank):
                first_tile = isinstance(i, int) and i == 0
                if first_tile:
                    turn(0, 0)
                dve.wait_ge(summed, 2 * i + 2)
                dve.wait_ge(silu_done, i + 1)
                after(dve, h_turned, i - 2)
                dve.tensor_tensor(hidden[:, u], silu[:, u], bank_v[bank][:], ALU.mult).then_inc(hidden_done, 1)
                if not (isinstance(i, int) and i == TILES - 1):
                    turn(i + 1, (u + 1) % U)
                if not first_tile:
                    result_out(i - 1, (u + 2) % U)
            every_tile(dve, body)
            result_out(TILES - 1, (TILES - 1) % U)

        @block.gpsimd
        def _(pool):
            def body(i, u, bank):
                pool.wait_ge(result_done, i + 1)
                after(pool, stored, 16 * i)
                pool.sem_inc(pool_waited, 1)
                pool.dma_start(slot_out[bass.ds(i * 128, 128), :], result[:, u]).then_inc(stored, 16)
            every_tile(pool, body)
            pool.wait_ge(stored, 16 * TILES)


def stage_combine(nc, x1, slots, weights, slot_out, out):
    with ExitStack() as ctx:
        def sem(name):
            return ctx.enter_context(nc.semaphore("c_" + name))

        U = 8
        got = ctx.enter_context(nc.sbuf_tensor("got", [T, U, 2, D], F32))
        gathered = [sem(f"gathered{u}") for u in range(U)]
        half = sem("half")
        summed = sem("summed")
        stored = sem("stored")
        block = ctx.enter_context(nc.Block())

        @block.gpsimd
        def _(pool):
            for b in range(BATCH):
                if b >= U:
                    pool.wait_ge(summed, b - U + 1)
                for c in range(2):
                    pool.indirect_dma_start(
                        out=got[:, b % U, c, :], out_offset=None, in_=slot_out,
                        in_offset=bass.IndirectOffsetOnAxis(ap=slots[:, c, b:b + 1], axis=0)
                    ).then_inc(gathered[b % U], 16)

        @block.vector
        def _(dve):
            for b in range(BATCH):
                dve.wait_ge(gathered[b % U], 32 * (b // U + 1))
                dve.scalar_tensor_tensor(x1[:, b, :], got[:, b % U, 0], weights[:, 0, b:b + 1], x1[:, b, :],
                                         ALU.mult, ALU.add).then_inc(half, 1)
                dve.wait_ge(half, b + 1)
                dve.scalar_tensor_tensor(x1[:, b, :], got[:, b % U, 1], weights[:, 1, b:b + 1], x1[:, b, :],
                                         ALU.mult, ALU.add).then_inc(summed, 1)

        @block.sync
        def _(sp):
            for b in range(0, BATCH, 4):
                sp.wait_ge(summed, b + 4)
                sp.dma_start(out[b:b + 4].rearrange("b t d -> t b d"), x1[:, b:b + 4, :]).then_inc(stored, 16)
            sp.wait_ge(stored, 16 * BATCH // 4)


def decoder_layer(nc, w, out):
    with ExitStack() as ctx:
        def sb(name, shape, dt=F32):
            return ctx.enter_context(nc.sbuf_tensor(name, shape, dt))

        x1 = sb("residual", [T, BATCH, D])
        moments_kept = sb("moments_kept", [T, BATCH, 3])
        logits = sb("logits", [T, BATCH, E])
        slots = sb("slots", [T, 2, BATCH], U32)
        slot_f = sb("slot_f", [T, 2, BATCH])
        weights = sb("weights", [T, 2, BATCH])
        tile_expert = sb("tile_expert", [1, TILES], I32)
        zeros = sb("zeros", [128, D])
        slot_rows = nc.dram_tensor("slot_rows", (TILES * 128, D), F32, kind="Internal").ap()
        slot_out = nc.dram_tensor("slot_out", (TILES * 128, D), F32, kind="Internal").ap()
        zeroed = ctx.enter_context(nc.semaphore("zeroed"))
        blank = ctx.enter_context(nc.semaphore("blank"))
        w1_loaded = ctx.enter_context(nc.semaphore("w1_loaded"))
        w2_loaded = ctx.enter_context(nc.semaphore("w2_loaded"))

        stage_mixer(nc, w, w["x"], x1, zeros, blank, slot_rows, zeroed)
        w1 = sb("expert_w1", [128, E, CC, 2 * F])
        stage_attention(nc, w, x1, moments_kept, logits, w1, w1_loaded)
        w2 = sb("expert_w2", [128, E, FC, D])
        ident = sb("eident", [128, 128])
        stage_routing(nc, w, x1, moments_kept, logits, slots, slot_f, weights, tile_expert, slot_rows, zeroed, w2, ident, w2_loaded)
        stage_experts(nc, w1, w1_loaded, w2, ident, w2_loaded, tile_expert, slot_rows, slot_out)
        stage_combine(nc, x1, slots, weights, slot_out, out)


def blocks(a):
    import numpy as np
    return np.ascontiguousarray(a.reshape(-1, 128, a.shape[-1]).transpose(1, 0, 2))


def padded(a, rows, cols):
    import numpy as np
    out = np.zeros((rows, cols), a.dtype)
    out[:a.shape[0], :a.shape[1]] = a
    return out


def level_masks():
    import numpy as np
    s, out = np.arange(T)[:, None], np.zeros((T, 5, T // 2), np.int32)
    for lv in range(1, 6):
        half = 1 << (lv - 1)
        t = np.arange(T)
        t = t[(t // half % 2 == 1) & (t // half * half + half <= T)][None, :]
        out[:, lv - 1, :t.shape[1]] = (s // half % 2 == 0) & (t // half == s // half + 1)
    return out


def laid_out(inputs):
    import numpy as np
    i = {n: np.asarray(a) for n, a in inputs.items()}
    p = {n[8:]: a for n, a in i.items() if n.startswith("L0_attn_")}
    lr = p["W_x1"].shape[0] // BRANCHES
    x2 = np.zeros((128, BRANCHES, D), np.float32)
    for b in range(BRANCHES):
        rows = (b % 4) * lr
        x2[rows:rows + lr, b] = p["W_x2"][:, b * lr:(b + 1) * lr].T
    out = {
        "x": i["x"],
        "x1": blocks(padded(p["W_x1"].T, D, 256)), "x2": x2,
        "r": blocks(p["W_r"].T), "k": blocks(p["W_k"].T), "a": blocks(padded(p["A_w"].T, D, 128)),
        "b": padded(p["B_w"].T, 128, 128), "v": blocks(p["W_v"].T), "g": blocks(p["W_g"].T),
        "o": blocks(p["W_o"].T), "mu_x": p["mu_x"].reshape(CC, 128).T,
        "x_bias": p["x_bias"].reshape(BRANCHES, CC, 128).transpose(2, 0, 1),
        "b_w": p["b_w"].reshape(128, 1), "bonus": p["bonus"].reshape(128, 1),
        "gn_w": np.broadcast_to(p["gn_weight"], (T, 256)), "gn_b": np.broadcast_to(p["gn_bias"], (T, 256)),
        "masks": level_masks(), "diagonal": np.eye(T, dtype=np.int32), "ident": np.eye(T, dtype=np.float32),
    }
    a = {n[9:]: v for n, v in i.items() if n.startswith("L0_xattn_")}

    def by_channel(v):
        return v.reshape(*v.shape[:-1], NH, 16).swapaxes(-1, -2).reshape(v.shape)

    def halves(v):
        return v.reshape(2, KC, -1).transpose(1, 0, 2)

    out.update({
        "ctx_t": i["ctx_768"].transpose(0, 2, 1), "xq": blocks(by_channel(a["Wq"])),
        "xk": halves(by_channel(a["Wk"])), "xv": halves(a["Wv"]), "xo": blocks(a["Wo"]),
        "xbq": by_channel(a["bq"]).reshape(CC, 128).T, "xbk": by_channel(a["bk"]).reshape(CC, 128).T,
        "xbv": np.broadcast_to(a["bv"], (128, D)), "xbo": np.broadcast_to(a["bo"], (T, D)),
        "w1": i["L0_ffn_W1"].transpose(2, 0, 1).reshape(CC, 128, E, 2 * F).transpose(1, 2, 0, 3),
        "w2": i["L0_ffn_W2"].transpose(2, 0, 1).reshape(FC, 128, E, D).transpose(1, 2, 0, 3),
        "router": blocks(i["L0_ffn_Wr"].T), "before": np.triu(np.ones((T, T), np.float32), 1),
        "iota_e": np.broadcast_to(np.arange(E, dtype=np.float32), (T, E)),
        "iota_full": np.broadcast_to(128 * np.arange(EXPERT_TILES, dtype=np.float32), (T, EXPERT_TILES)),
        "iota_tile": np.broadcast_to(np.arange(TILES, dtype=np.float32), (T, TILES)),
        "ident128": np.eye(128, dtype=np.float32),
    })
    return {n: np.ascontiguousarray(a) for n, a in out.items()}


def kernel(**inputs):
    import concourse.bacc as bacc
    from concourse.bass_utils import run_bass_kernel_spmd

    nc = bacc.Bacc("TRN2", target_bir_lowering=False, num_devices=1)
    arrays = laid_out(inputs)
    w = {n: nc.dram_tensor(f"in_{n}", a.shape, mybir.dt.from_np(a.dtype), kind="ExternalInput").ap()
         for n, a in arrays.items()}
    out = nc.dram_tensor("out", (BATCH, T, D), F32, kind="ExternalOutput").ap()
    decoder_layer(nc, w, out)
    result = run_bass_kernel_spmd(nc, [{f"in_{n}": a for n, a in arrays.items()}], core_ids=[0])
    return result.results[0]["out"]
```
